# Optimizing a Trainium2 kernel written in Bass

```python
import numpy as np
import jax
import jax.numpy as jnp

def _softmax(x, axis=-1):
    return jax.nn.softmax(x, axis=axis)

def _gelu(x):
    return jax.nn.gelu(x, approximate=True)

def _silu(x):
    return jax.nn.silu(x)

def _sigmoid(x):
    return jax.nn.sigmoid(x)

def _layernorm(x, axis=-1, eps=1e-05):
    m = jnp.mean(x, axis=axis, keepdims=True)
    v = jnp.var(x, axis=axis, keepdims=True)
    return (x - m) / jnp.sqrt(v + eps)

def _scatter_add(tgt, idx, src, axis=0):
    return tgt.at[idx].add(src)

def _segment_sum(src, seg, n):
    return jax.ops.segment_sum(src, seg, n)
kernel_name = 'mk_gnn_resnorm_d4_gnn_r8_b4323e'

def setup_inputs(seed: int=0):
    np.random.seed(seed)
    _w = jnp.asarray

    def _rec_inputs():
        import jax
        import jax.numpy as jnp
        _gk = jax.random.key(seed)
        x = -0.0009044 + 1 * jax.random.normal(jax.random.fold_in(_gk, 1), (12500, 32), jnp.float32)
        _s = jax.random.randint(jax.random.fold_in(_gk, 2), (200000,), 0, 12500, jnp.int32)
        _d = jax.random.randint(jax.random.fold_in(_gk, 3), (200000,), 0, 12500, jnp.int32)
        _loop = jnp.arange(12500, dtype=jnp.int32)
        src = jnp.concatenate([_s, _d, _loop])
        dst = jnp.concatenate([_d, _s, _loop])
        _o = jnp.argsort(dst, stable=True)
        src = src[_o]
        dst = dst[_o]
        edge_attr_32 = 0.000196303 + 1.00016 * jax.random.normal(jax.random.fold_in(_gk, 11), (412500, 32), jnp.float32)
        return (x, src, dst, edge_attr_32)
    x, src, dst, edge_attr_32 = _rec_inputs()

    def _L0_gnn_setup():
        import jax, jax.numpy as jnp
        import numpy as np
        N_NODES = 6250
        N_EDGES = 100000
        X_DIM = 32
        E_DIM = 32
        HID = 64
        OUT = 32
        key = jax.random.key(seed)
        ks = jax.random.split(key, 6)
        x = jax.random.normal(ks[0], (N_NODES, X_DIM), dtype=jnp.float32)
        edge_index = jax.random.randint(ks[1], (2, N_EDGES), 0, N_NODES, dtype=jnp.int64)
        edge_attr = jax.random.normal(ks[2], (N_EDGES, E_DIM), dtype=jnp.float32)
        in_dim = 2 * X_DIM + E_DIM
        W1 = jax.random.normal(ks[3], (in_dim, HID), dtype=jnp.float32) * (1.0 / np.sqrt(in_dim))
        b1 = jnp.zeros((HID,), dtype=jnp.float32)
        W2 = jax.random.normal(ks[4], (HID, OUT), dtype=jnp.float32) * (1.0 / np.sqrt(HID))
        b2 = jnp.zeros((OUT,), dtype=jnp.float32)
        return {'x': x, 'edge_index': edge_index, 'edge_attr': edge_attr, 'W1': W1, 'b1': b1, 'W2': W2, 'b2': b2}
    _L0_gnn_all = _L0_gnn_setup()
    _L0_gnn_in = {k: v for k, v in _L0_gnn_all.items() if k in ('W1', 'b1', 'W2', 'b2')}
    del _L0_gnn_all

    def _L1_gnn_setup():
        import jax, jax.numpy as jnp
        import numpy as np
        N_NODES = 6250
        N_EDGES = 200000
        D_FEAT = 32
        key = jax.random.key(seed)
        kx, ke = jax.random.split(key)
        x = jax.random.normal(kx, (N_NODES, D_FEAT), dtype=jnp.float32)
        edge_index = jax.random.randint(ke, (2, N_EDGES), 0, N_NODES, dtype=jnp.int64)
        return {'x': x, 'edge_index': edge_index, 'num_nodes': N_NODES}
    _L1_gnn_all = _L1_gnn_setup()
    _L1_gnn_in = {k: v for k, v in _L1_gnn_all.items() if k in ()}
    del _L1_gnn_all

    def _L2_gnn_setup():
        import jax, jax.numpy as jnp
        import numpy as np
        N_NODES = 6250
        DEG = 16
        N_HEAD = 4
        F_IN = 32
        F_OUT = 32
        key = jax.random.key(seed)
        k_h, k_w, k_fw, k_fb = jax.random.split(key, 4)
        h = jax.random.normal(k_h, (N_NODES, F_IN), dtype=jnp.float32)
        src = jnp.repeat(jnp.arange(N_NODES, dtype=jnp.int64), DEG)
        offs = (jnp.arange(DEG, dtype=jnp.int64) + 1) * 97
        dst = (src.reshape(N_NODES, DEG) + offs[None, :]).reshape(-1) % N_NODES
        edge_index = jnp.stack([src, dst], axis=0)
        gain = 1.414
        bound_w = gain * np.sqrt(6.0 / (F_IN + F_OUT))
        w = jax.random.uniform(k_w, (N_HEAD, F_IN, F_OUT), jnp.float32, -bound_w, bound_w)
        bound_fc = np.sqrt(1.0 / (2 * F_OUT))
        fc_w = jax.random.uniform(k_fw, (1, 2 * F_OUT), jnp.float32, -bound_fc, bound_fc)
        fc_b = jax.random.uniform(k_fb, (1,), jnp.float32, -bound_fc, bound_fc)
        bias = jnp.zeros((F_OUT,), jnp.float32)
        return {'h': h, 'edge_index': edge_index, 'w': w, 'fc_w': fc_w, 'fc_b': fc_b, 'bias': bias}
    _L2_gnn_all = _L2_gnn_setup()
    _L2_gnn_in = {k: v for k, v in _L2_gnn_all.items() if k in ('w', 'fc_w', 'fc_b', 'bias')}
    del _L2_gnn_all

    def _L3_gnn_setup():
        import jax, jax.numpy as jnp
        import numpy as np
        N_NODES = 12500
        N_EDGES = 200000
        IN_C, HID_C, OUT_C = (32, 64, 32)

        def _sage_conv(x, src, dst, W_l, b_l, W_r):
            n = x.shape[0]
            agg = jax.ops.segment_sum(x[src], dst, num_segments=n)
            cnt = jax.ops.segment_sum(jnp.ones_like(dst, dtype=x.dtype), dst, num_segments=n)
            agg = agg / jnp.maximum(cnt, 1.0)[:, None]
            return agg @ W_l + b_l + x @ W_r
        key = jax.random.key(seed)
        ks = jax.random.split(key, 8)
        x = jax.random.normal(ks[0], (N_NODES, IN_C), dtype=jnp.float32)
        edge_index = jax.random.randint(ks[1], (2, N_EDGES), 0, N_NODES, dtype=jnp.int64)
        s = 1.0 / np.sqrt(IN_C)
        W1_l = jax.random.uniform(ks[2], (IN_C, HID_C), jnp.float32, -s, s)
        W1_r = jax.random.uniform(ks[3], (IN_C, HID_C), jnp.float32, -s, s)
        b1 = jnp.zeros((HID_C,), jnp.float32)
        s2 = 1.0 / np.sqrt(HID_C)
        W2_l = jax.random.uniform(ks[4], (HID_C, OUT_C), jnp.float32, -s2, s2)
        W2_r = jax.random.uniform(ks[5], (HID_C, OUT_C), jnp.float32, -s2, s2)
        b2 = jnp.zeros((OUT_C,), jnp.float32)
        return {'x': x, 'edge_index': edge_index, 'W1_l': W1_l, 'b1': b1, 'W1_r': W1_r, 'W2_l': W2_l, 'b2': b2, 'W2_r': W2_r}
    _L3_gnn_all = _L3_gnn_setup()
    _L3_gnn_in = {k: v for k, v in _L3_gnn_all.items() if k in ('W1_l', 'b1', 'W1_r', 'W2_l', 'b2', 'W2_r')}
    del _L3_gnn_all
    return {'x': x, 'src': src, 'dst': dst, 'edge_attr_32': edge_attr_32, 'L0_gnn_W1': _L0_gnn_in['W1'], 'L0_gnn_b1': _L0_gnn_in['b1'], 'L0_gnn_W2': _L0_gnn_in['W2'], 'L0_gnn_b2': _L0_gnn_in['b2'], 'L2_gnn_w': _L2_gnn_in['w'], 'L2_gnn_fc_w': _L2_gnn_in['fc_w'], 'L2_gnn_fc_b': _L2_gnn_in['fc_b'], 'L2_gnn_bias': _L2_gnn_in['bias'], 'L3_gnn_W1_l': _L3_gnn_in['W1_l'], 'L3_gnn_b1': _L3_gnn_in['b1'], 'L3_gnn_W1_r': _L3_gnn_in['W1_r'], 'L3_gnn_W2_l': _L3_gnn_in['W2_l'], 'L3_gnn_b2': _L3_gnn_in['b2'], 'L3_gnn_W2_r': _L3_gnn_in['W2_r']}

def reference(x, src, dst, edge_attr_32, L0_gnn_W1, L0_gnn_b1, L0_gnn_W2, L0_gnn_b2, L2_gnn_w, L2_gnn_fc_w, L2_gnn_fc_b, L2_gnn_bias, L3_gnn_W1_l, L3_gnn_b1, L3_gnn_W1_r, L3_gnn_W2_l, L3_gnn_b2, L3_gnn_W2_r):
    import jax
    import jax.numpy as jnp

    def _L0_gnn_ref(x, edge_index, edge_attr, W1, b1, W2, b2):
        import jax, jax.numpy as jnp
        import numpy as np
        N_NODES = 6250
        N_EDGES = 100000
        X_DIM = 32
        E_DIM = 32
        HID = 64
        OUT = 32
        num_nodes = x.shape[0]
        rol, col = (edge_index[0], edge_index[1])
        e_feat = jnp.concatenate([x[rol], x[col], edge_attr], axis=-1)
        h = jax.nn.relu(e_feat @ W1 + b1)
        v = h @ W2 + b2
        x_cand = jax.ops.segment_max(v, col, num_segments=num_nodes)
        return jnp.maximum(x_cand, x[:, -v.shape[-1]:])

    def _L1_gnn_ref(x, edge_index, num_nodes):
        import jax, jax.numpy as jnp
        import numpy as np
        N_NODES = 6250
        N_EDGES = 200000
        D_FEAT = 32
        src = edge_index[0]
        dst = edge_index[1]
        msgs = x[src]
        out = jax.ops.segment_sum(msgs, dst, num_segments=num_nodes)
        return out

    def _L2_gnn_ref(h, edge_index, w, fc_w, fc_b, bias):
        import jax, jax.numpy as jnp
        import numpy as np
        N_NODES = 6250
        DEG = 16
        N_HEAD = 4
        F_IN = 32
        F_OUT = 32
        n_head, f_in, f_out = w.shape
        n = h.shape[0]
        src, dst = (edge_index[0], edge_index[1])
        hp = jnp.einsum('nf,hfo->hno', h, w)
        w_src = fc_w[0, :f_out]
        w_dst = fc_w[0, f_out:]
        a_src = jnp.einsum('hnf,f->hn', hp, w_src)
        a_dst = jnp.einsum('hnf,f->hn', hp, w_dst)
        e = a_src[:, src] + a_dst[:, dst] + fc_b[0]
        e = jax.nn.leaky_relu(e, negative_slope=0.2)
        seg_max = jax.ops.segment_max(e.T, src, num_segments=n)
        e = jnp.exp(e - seg_max.T[:, src])
        seg_sum = jax.ops.segment_sum(e.T, src, num_segments=n)
        att = e / seg_sum.T[:, src]
        msg = att[:, :, None] * hp[:, dst, :]
        agg = jax.vmap(lambda m: jax.ops.segment_sum(m, src, num_segments=n))(msg)
        out = agg.mean(axis=0) + bias
        return out

    def _L3_gnn_ref(x, edge_index, W1_l, b1, W1_r, W2_l, b2, W2_r):
        import jax, jax.numpy as jnp
        import numpy as np
        N_NODES = 12500
        N_EDGES = 200000
        IN_C, HID_C, OUT_C = (32, 64, 32)

        def _sage_conv(x, src, dst, W_l, b_l, W_r):
            n = x.shape[0]
            agg = jax.ops.segment_sum(x[src], dst, num_segments=n)
            cnt = jax.ops.segment_sum(jnp.ones_like(dst, dtype=x.dtype), dst, num_segments=n)
            agg = agg / jnp.maximum(cnt, 1.0)[:, None]
            return agg @ W_l + b_l + x @ W_r
        src, dst = (edge_index[0], edge_index[1])
        h = jax.nn.relu(_sage_conv(x, src, dst, W1_l, b1, W1_r))
        out = _sage_conv(h, src, dst, W2_l, b2, W2_r)
        return out
    edge_index = jnp.stack([src, dst])
    x = _layernorm(x + _L0_gnn_ref(x, edge_index, edge_attr_32, L0_gnn_W1, L0_gnn_b1, L0_gnn_W2, L0_gnn_b2), axis=-1)
    x = _layernorm(x + _L1_gnn_ref(x, edge_index, 12500), axis=-1)
    x = _layernorm(x + _L2_gnn_ref(x, edge_index, L2_gnn_w, L2_gnn_fc_w, L2_gnn_fc_b, L2_gnn_bias), axis=-1)
    x = _layernorm(x + _L3_gnn_ref(x, edge_index, L3_gnn_W1_l, L3_gnn_b1, L3_gnn_W1_r, L3_gnn_W2_l, L3_gnn_b2, L3_gnn_W2_r), axis=-1)
    return x

_drawn_inputs = setup_inputs


def setup_inputs(seed=0):
    import zlib

    import numpy as np

    out = dict(_drawn_inputs(seed))
    spreads = {'L0_gnn_b1': (0.0, 0.1),
     'L0_gnn_b2': (0.0, 0.1),
     'L2_gnn_bias': (0.0, 0.1),
     'L3_gnn_b1': (0.0, 0.1),
     'L3_gnn_b2': (0.0, 0.1)}
    factors = {}
    for name, (base, spread) in spreads.items():
        noise = np.random.default_rng([zlib.crc32(name.encode()), seed]).standard_normal(out[name].shape)
        drawn = base * np.exp(spread * noise) if base else spread * noise
        out[name] = jnp.asarray(drawn.astype(out[name].dtype))
    for name, factor in factors.items():
        out[name] = (out[name] * factor).astype(out[name].dtype)
    return out
```

```python
from contextlib import ExitStack

import concourse.bass as bass
from concourse import mybir

ALU = mybir.AluOpType
ACT = mybir.ActivationFunctionType
AX = mybir.AxisListType
F32 = mybir.dt.float32
I32 = mybir.dt.int32

P = 128
TILES = 16
CHUNK = P * TILES
WIN = 96
EPS = 1e-5
START = -(2.0 ** 100)
EMPTY = 1e30


def sizes(n_nodes, n_edges):
    chunks = -(-n_edges // CHUNK)
    chunks += chunks % 2
    steps = chunks + n_nodes // WIN + 1
    return chunks, steps + steps % 2


def gnn(nc, x, src, dst, edge_attr, W1, b1, W2, b2, gat_w, fc_w, fc_b, gat_bias,
        S1l, sb1, S1r, S2l, sb2, S2r, out, n_edges):
    N, D = out.shape
    NP = x.shape[0]
    NB = NP // P
    NT = NP + P
    HID = W1.shape[1]
    H = gat_w.shape[0]
    CH, STEPS = sizes(N, n_edges)
    TAB = -(-STEPS // P)
    TW = D + H
    HALF = CHUNK // 4
    assert D == 32 and HID == 64 and H * D == P and NP % P == 0

    with ExitStack() as ctx:
        def sb(name, shape, dt=F32):
            return ctx.enter_context(nc.sbuf_tensor(name, shape, dt))

        def sem(name):
            return ctx.enter_context(nc.semaphore(name))

        def slots(name):
            return [sem(f"{name}{k}") for k in range(2)]

        def dram(name, shape, dt=F32):
            return nc.dram_tensor(name, shape, dt, kind="Internal").ap()

        plan_d = dram("plan_d", (2, TAB * P), I32)
        count_d = dram("count_d", (1, 1), I32)
        q_d = dram("q_d", (NT, HID))
        x1_d = dram("x1_d", (NP, D))
        x2_d = dram("x2_d", (NP, TW))
        gat_d = dram("gat_d", (NT, 2 * H))
        edges_d = dram("edges_d", (CH * CHUNK, TW))
        x3_d = dram("x3_d", (NP, D))
        p_d = dram("p_d", (NP, D))

        acc = sb("acc", [P, NT])
        xn = sb("xn", [P, NB, D])
        rdeg = sb("rdeg", [P, NB])
        ident = sb("ident", [P, P])
        iota_w = sb("iota_w", [P, WIN])
        iota_p = sb("iota_p", [P, 1])
        base_f = sb("base_f", [P, TAB * P])
        plan = sb("plan", [1, 2, TAB * P], I32)
        count = sb("count", [1, 1], I32)
        small = sb("small", [P, 640])
        carry = sb("carry", [D, CH + 1])
        WORK = 31100
        work = sb("work", [P, WORK])
        yn = work[:, WORK - NB * TW:WORK].rearrange("p (b f) -> p b f", f=TW)

        class Arena:
            def __init__(self):
                self.at = 0

            def __call__(self, parts, *dims, dt=F32):
                n = 1
                for d in dims:
                    n *= d
                v = work[0:parts, self.at:self.at + n]
                self.at += n + n % 2
                assert self.at <= WORK, self.at
                if dt is not F32:
                    v = v.bitcast(dt)
                if len(dims) == 2:
                    v = v.rearrange("p (a b) -> p a b", a=dims[0])
                return v

        bank = [ctx.enter_context(nc.psum_tensor(f"bank{i}", [P, 512], F32)) for i in range(8)]

        at = [0]

        def param(parts, n):
            v = small[0:parts, at[0]:at[0] + n]
            at[0] += n
            assert at[0] <= 640
            return v

        w1_edge = param(2 * D, HID)
        w1_dst = param(D, HID)
        w2 = param(HID, D)
        b1_col = param(HID, 1)
        b2_row = param(P, D)
        wa = param(D, 2 * H)
        fc_b_col = param(P, 1)
        gat_bias_row = param(P, D)
        w_heads = param(P, P)
        s1 = param(2 * D, HID)
        sb1_col = param(HID, 1)
        s2 = param(HID, 2 * D)
        sb2_row = param(P, D)
        eps_col = param(P, 1)

        block = ctx.enter_context(nc.Block())

        arrived = sem("arrived")
        meetings = {}

        def meet(eng, who):
            meetings[who] = meetings.get(who, 0) + 1
            eng.drain().then_inc(arrived, 1)
            eng.wait_ge(arrived, 5 * meetings[who])

        held = sem("held")

        def hold(eng):
            eng.sem_inc(held, 1)

        def steps(eng, body):
            n = eng.value_load(count[0:1, 0:1], min_val=CH, max_val=STEPS)
            with eng.Fori(0, CH // 2) as it:
                body(it)
            with eng.Fori(CH // 2, STEPS // 2) as it:
                with eng.If(n > 2 * it):
                    body(it)

        def chunk_of(eng, it, k):
            return eng.value_load(plan[0:1, 0, bass.ds(2 * it + k, 1)], min_val=0, max_val=CH - 1)

        def base_of(eng, it, k):
            return eng.value_load(plan[0:1, 1, bass.ds(2 * it + k, 1)], min_val=0, max_val=NP)

        def edge_slice(flat, c, first=0):
            return flat[bass.ds(c * CHUNK + first, CHUNK)].rearrange("(p t) -> p t", t=TILES)

        def rows(table):
            return table[0:NP, :].rearrange("(b p) f -> p b f", p=P)

        GROUP = 14
        GROUPS = NB // GROUP
        FOURS = [(b, min(4, NB - b)) for b in range(0, NB, 4)]
        SEVENS = NB // 7
        assert NB % GROUP == 0

        class Own:

            def __init__(self, eng, name, per=0, it=None):
                self.eng, self.s, self.n = eng, sem(name), 0

            def __call__(self, ins):
                self.n += 1
                ins.then_inc(self.s, 1)
                self.eng.wait_ge(self.s, self.n)

        s_in = sem("inputs_loaded")
        s_const = sem("constants_made")
        s_zero = sem("heads_zeroed")
        s_wa = sem("attention_rows_made")
        s_plan_in, s_plan_made = sem("plan_loaded"), sem("plan_made")
        s_plan_b = sem("plan_broadcast")
        s_plan_st, s_plan_ld = sem("plan_stored"), sem("plan_reloaded")
        names = "abcdefgh"
        s_turn = [sem(f"turned_{c}") for c in names]
        s_evac = [sem(f"evacuated_{c}") for c in names]
        s_turn_n, s_evac_n = {}, {}
        s_out = sem("stored")
        stored = [0]

        def store(eng, to, of):
            eng.dma_start(to, of).then_inc(s_out, 16)
            stored[0] += 16

        def pe_groups(i, n, fill):
            for g in range(n):
                if g >= 2:
                    nc.tensor.wait_ge(s_evac[i], g - 1)
                fill(g, bank[g % 2]).then_inc(s_turn[i], 1)

        def take_groups(eng, i, n, empty):
            for g in range(n):
                eng.wait_ge(s_turn[i], g + 1)
                empty(g, bank[g % 2]).then_inc(s_evac[i], 1)

        def turn_to_nodes(parts, of):
            def fill(g, b):
                for j in range(GROUP):
                    n0 = (g * GROUP + j) * P
                    m = nc.tensor.transpose(b[:, j * parts:(j + 1) * parts], of[0:parts, n0:n0 + P],
                                            ident[0:parts, 0:parts])
                return m
            return fill

        def turn_to_features(width, of):
            def fill(g, b):
                b0, n = FOURS[g]
                for j in range(n):
                    m = nc.tensor.transpose(b[0:width, j * P:(j + 1) * P], of(b0 + j), ident[:, :])
                return m
            return fill

        def empty_to(eng_copy, to, width):
            def empty(g, b):
                b0, n = FOURS[g]
                return eng_copy(to[0:width, b0 * P:(b0 + n) * P], b[0:width, 0:n * P])
            return empty

        act_copy = lambda o, i: nc.scalar.activation(o, i, ACT.Copy)

        a = Arena()
        xe = [a(P, TILES, 2 * D) for _ in range(2)]
        idx = [a(P, TILES, dt=I32) for _ in range(2)]
        dst_i = [a(P, TILES, dt=I32) for _ in range(2)]
        next_i = [a(P, TILES, dt=I32) for _ in range(2)]
        last_f = a(P, TILES)
        key_f = a(P, TILES)
        win_f = a(P, WIN)
        win_p = a(P, 1)
        onehot = [a(P, TILES, WIN) for _ in range(2)]
        LIN = a.at
        row_i = [a(WIN, CHUNK + 2, dt=I32) for _ in range(2)]
        onehot_t = [a(WIN, CHUNK) for _ in range(2)]
        q_win = [a(WIN, HID) for _ in range(2)]
        row_f = a(D, CHUNK + 2)
        starts = [a(D, CHUNK) for _ in range(2)]
        xe_t = [a(2 * D, CHUNK) for _ in range(2)]
        hid_t = a(HID, CHUNK)
        run = [a(D, CHUNK) for _ in range(2)]
        first = a(D, 1)
        run_e = a(P, TILES, D + 1)

        l0 = {n: sem("mlp_" + n) for n in (
            "xe_turned", "xe_t", "hidden", "relu", "values", "scanned", "run_turned", "run_e",
            "picked", "added", "ones", "carry0", "starts", "row_f", "gather_turn", "chain")}
        l0_a, l0_b, l0_g = slots("mlp_near_loaded"), slots("mlp_far_loaded"), slots("mlp_gathered")

        a = Arena()
        a.at = LIN
        xg = [a(P, TILES, D + 1) for _ in range(2)]

        a = Arena()
        a.at = LIN
        xa = [a(P, TILES, TW) for _ in range(2)]
        row4_i = [a(H, CHUNK + 2, dt=I32) for _ in range(2)]
        row4_f = a(H, CHUNK + 2)
        starts4 = [a(H, CHUNK) for _ in range(2)]
        ad_t = [a(H, CHUNK) for _ in range(2)]
        run4 = [a(H, CHUNK) for _ in range(2)]
        first4 = a(H, 1)
        run4_e = a(P, TILES, H)
        a = Arena()
        a.at = LIN
        a(P, 2 * TILES * TW)
        row2_i = [a(WIN, CHUNK, dt=I32) for _ in range(2)]
        onehot2_t = [a(WIN, CHUNK) for _ in range(2)]
        gat_win = [a(WIN, 2 * H) for _ in range(2)]
        logit = [a(P, TILES, H) for _ in range(2)]
        tmp4 = a(P, TILES, H)
        weight = [a(P, TILES, H) for _ in range(2)]
        msg = a(P, TILES, P)
        den = a(H, NT)

        def gathers(g, name, table, to, width, ready, ready_n, turn, done):
            def body(it):
                for k in range(2):
                    g.wait_ge(ready[k], (it + 1) * (16 * ready_n))
                    g.sem_inc(turn, 1)
                    for t in range(TILES):
                        g.indirect_dma_start(
                            to[k][:, t, 0:width], None, table,
                            bass.IndirectOffsetOnAxis(idx[k][:, t:t + 1], 0)).then_inc(done[k], 16)
            steps(g, body)

        lin = []
        for n in range(3):
            lin.append(dict(
                near=slots(f"sum{n}_idx_loaded"), far=slots(f"sum{n}_dst_loaded"),
                gathered=slots(f"sum{n}_gathered"), onehot=sem(f"sum{n}_onehot"),
                summed=sem(f"sum{n}_summed"), added=sem(f"sum{n}_added"),
                turn=sem(f"sum{n}_gather_turn"), chain=sem(f"sum{n}_chain"), ones=sem(f"sum{n}_ones")))
        g1 = {n: sem("gat_max_" + n) for n in (
            "turned", "ad_t", "row_f", "starts", "scanned", "run_turned", "run_e", "picked", "added",
            "gather_turn", "chain", "carry0")}
        g1_a, g1_b, g1_g, g1_s = (slots("gat_max_idx_loaded"), slots("gat_max_dst_loaded"),
                                  slots("gat_max_gathered"), slots("gat_max_stored"))
        g2 = {n: sem("gat_sum_" + n) for n in (
            "onehots", "spread", "logit", "weight", "msg", "summed", "added", "chain")}
        g2_l = slots("gat_sum_loaded")

        a = Arena()
        ends_i = a(1, 2, CH, dt=I32)
        more_i = a(1, CH, dt=I32)
        row_s = a(1, CH)
        zero_s = a(1, CH)
        start_s = a(1, 2, CH)
        val_s = a(1, CH)
        start_b = a(P, 2, CH)
        step_s = a(P, TAB)
        hit_s = a(P, CH)
        got_s = a(P, 2, TAB)
        got_i = a(P, 2, TAB, dt=I32)
        n_i = a(1, 1, dt=I32)
        ends_f = a(1, 2, CH)
        s_step = sem("step_numbers")

        def plan_gpsimd(g):
            g.iota(step_s, [[P, TAB]], base=0, channel_multiplier=1,
                   allow_small_or_imprecise_dtypes=True).then_inc(s_step, 1)
            g.wait_ge(s_plan_made, 1)
            g.partition_broadcast(start_b.rearrange("p a b -> p (a b)"),
                                  start_s.rearrange("p a b -> p (a b)")).then_inc(s_plan_b, 1)

        fc_rows = work[0:D, 8000:8000 + 2 * D]
        w_fho = work[0:D, 8100:8100 + P].rearrange("p (h o) -> p h o", h=H)
        wprod = work[0:D, 8300:8300 + P].rearrange("p (h o) -> p h o", h=H)
        base_i = work[:, 9000:9000 + TAB * P].bitcast(I32)
        q_n = work[:, 0:NB * HID].rearrange("p (b f) -> p b f", f=HID)
        zero_tail = work[:, NB * HID:NB * HID + HID]
        cen = work[:, 0:NB * D].rearrange("p (b f) -> p b f", f=D)
        sq = work[:, NB * D:2 * NB * D].rearrange("p (b f) -> p b f", f=D)
        mean = work[:, 2 * NB * D:2 * NB * D + NB]
        var = work[:, 2 * NB * D + NB:2 * NB * D + 2 * NB]
        rstd = work[:, 2 * NB * D + 2 * NB:2 * NB * D + 3 * NB]
        has = work[:, 2 * NB * D + 3 * NB:2 * NB * D + 4 * NB]
        MORE = 2 * NB * D + 4 * NB
        res_n = work[:, MORE:MORE + NB * D].rearrange("p (b f) -> p b f", f=D)
        hs_t = work[0:HID, MORE + NB * D:MORE + NB * D + NP]
        asd = sb("asd", [P, NB, 2 * H])
        gat_n = work[:, 0:NB * 2 * H].rearrange("p (b f) -> p b f", f=2 * H)
        gat_u = work[:, 1000:1000 + NB * H].rearrange("p (b f) -> p b f", f=H)
        p_n = cen
        s_tail = sem("zero_tail")
        s_norm = sem("normed")
        s_norm_n = {"sp": 0}
        s_asd = sem("attention_terms")
        s_gat_tab = sem("attention_table")
        s_p = sem("projected")
        s_ready = [sem(f"acc_zero{i}") for i in range(6)]

        s_terms, s_max_n, s_cat, s_hp, s_hs = (sem(n) for n in ("terms", "max_turned", "cat", "hid_made", "hid_relu"))
        s_pr, s_pr_out, s_fin, s_fin_out = (sem(n) for n in ("projections", "projections_out", "fin_turned", "fin_out"))
        s_sqrt = sem("sqrt")
        s_var = sem("variance")
        cat_n = work[:, 0:NB * 2 * D].rearrange("p (b f) -> p b f", f=2 * D)

        s_root = [0]
        s_asd_half = sem("attention_terms_half")

        s_dve_root = [0]
        heads_tmp = [work[:, MORE + 512 * i:MORE + 512 * (i + 1)] for i in range(2)]

        @block.gpsimd
        def _(g):
            g.memset(ident[:], 0.0).then_inc(s_const, 1)
            g.iota(iota_w[:], [[1, WIN]], base=0, channel_multiplier=0,
                   allow_small_or_imprecise_dtypes=True).then_inc(s_const, 1)
            g.iota(iota_p[:], [[0, 1]], base=0, channel_multiplier=1,
                   allow_small_or_imprecise_dtypes=True).then_inc(s_const, 1)
            g.memset(eps_col, EPS).then_inc(s_const, 1)
            g.wait_ge(s_const, 4)
            g.affine_select(out=ident[:], in_=ident[:], compare_op=ALU.not_equal, fill=1.0, base=0,
                            pattern=[[-1, P]], channel_multiplier=1).then_inc(s_const, 1)
            g.memset(w_heads, 0.0).then_inc(s_zero, 1)
            plan_gpsimd(g)
            meet(g, "pool")
            meet(g, "pool")
            gathers(g, "mlp", x, [v[:, :, 0:D] for v in xe], D, l0_a, 2, l0["gather_turn"], l0_g)
            meet(g, "pool")
            meet(g, "pool")
            gathers(g, "sum0", x1_d, xg, D, lin[0]["near"], 1, lin[0]["turn"], lin[0]["gathered"])
            meet(g, "pool")
            meet(g, "pool")
            gathers(g, "gat", x2_d, xa, TW, g1_a, 1, g1["gather_turn"], g1_g)
            meet(g, "pool")
            meet(g, "pool")
            meet(g, "pool")
            meet(g, "pool")
            gathers(g, "sum1", x3_d, xg, D, lin[1]["near"], 1, lin[1]["turn"], lin[1]["gathered"])
            meet(g, "pool")
            meet(g, "pool")
            gathers(g, "sum2", p_d, xg, D, lin[2]["near"], 1, lin[2]["turn"], lin[2]["gathered"])
            meet(g, "pool")
            meet(g, "pool")

        @block.sync
        def _(sp):
            ends = dst[1:1 + CH * CHUNK].rearrange("(c e) -> c e", e=CHUNK)
            with nc.allow_non_contiguous_dma(reason="one number per chunk"):
                sp.dma_start(ends_i[:, 0, :], ends[:, 0:1].rearrange("c o -> o c")).then_inc(s_plan_in, 16)
                sp.dma_start(ends_i[:, 1, :], ends[:, CHUNK - 1:CHUNK].rearrange("c o -> o c")).then_inc(s_plan_in, 16)
            sp.wait_ge(s_zero, 1)
            loads = [
                (xn[:], rows(x)),
                (w1_edge[0:D, :], W1[0:D, :]), (w1_dst, W1[D:2 * D, :]),
                (w1_edge[D:2 * D, :], W1[2 * D:3 * D, :]),
                (w2, W2), (s1[0:D, :], S1l), (s1[D:2 * D, :], S1r), (s2[:, 0:D], S2l), (s2[:, D:2 * D], S2r),
                (b1_col, b1.rearrange("(n o) -> n o", o=1)), (sb1_col, sb1.rearrange("(n o) -> n o", o=1)),
                (b2_row, b2.rearrange("(o n) -> o n", o=1).partition_broadcast(P)),
                (sb2_row, sb2.rearrange("(o n) -> o n", o=1).partition_broadcast(P)),
                (gat_bias_row, gat_bias.rearrange("(o n) -> o n", o=1).partition_broadcast(P)),
                (fc_b_col, fc_b.rearrange("(o n) -> o n", o=1).partition_broadcast(P)),
                (fc_rows, fc_w.partition_broadcast(D)),
                (w_fho, gat_w.rearrange("h f o -> f h o")),
            ] + [(w_heads[h * D:(h + 1) * D, h * D:(h + 1) * D], gat_w[h]) for h in range(H)]
            for to, of in loads:
                sp.dma_start(to, of).then_inc(s_in, 16)
            sp.wait_ge(s_in, 16 * len(loads))
            sp.wait_ge(s_plan_made, 2)
            with nc.allow_non_contiguous_dma(reason="plan, one number per step"):
                for r in range(2):
                    sp.dma_start(plan_d[r].rearrange("(j p) -> p j", p=P), got_i[:, r, :]).then_inc(s_plan_st, 16)
            sp.wait_ge(s_plan_st, 32)
            sp.dma_start(plan[:], plan_d.rearrange("(o r) s -> o r s", o=1)).then_inc(s_plan_ld, 16)
            sp.dma_start(base_i, plan_d[1:2, :].partition_broadcast(P)).then_inc(s_plan_ld, 16)
            sp.wait_ge(s_plan_ld, 32)
            meet(sp, "sp")

            sp.wait_ge(s_evac[1], SEVENS)
            sp.wait_ge(s_tail, 1)
            store(sp, rows(q_d), q_n)
            store(sp, q_d[NP:NT, :], zero_tail[:, 0:HID])
            store(sp, gat_d[NP:NT, :], zero_tail[:, 0:2 * H])
            sp.wait_ge(s_out, stored[0])
            meet(sp, "sp")

            def mlp_loads(it):
                for k in range(2):
                    c, b = chunk_of(sp, it, k), base_of(sp, it, k)
                    sp.wait_ge(l0["xe_turned"], it * 8 + 4 * (k + 1))
                    sp.dma_start(idx[k], edge_slice(src, c)).then_inc(l0_a[k], 16)
                    sp.dma_start(xe[k][:, :, D:2 * D],
                                 edge_attr[bass.ds(c * CHUNK, CHUNK), :].rearrange("(p t) f -> p t f", t=TILES)
                                 ).then_inc(l0_a[k], 16)
                    sp.wait_ge(l0["added"], it * 2 + (k + 1))
                    sp.dma_start(dst_i[k], edge_slice(dst, c, 1)).then_inc(l0_b[k], 16)
                    sp.dma_start(next_i[k], edge_slice(dst, c, 2)).then_inc(l0_b[k], 16)
                    sp.dma_start(row_i[k][:, 0:CHUNK + 1],
                                 dst[bass.ds(c * CHUNK, CHUNK + 1)].rearrange("(o e) -> o e", o=1)
                                 .partition_broadcast(WIN)).then_inc(l0_b[k], 16)
                    sp.dma_start(q_win[k], q_d[bass.ds(b, WIN), :]).then_inc(l0_b[k], 16)
            steps(sp, mlp_loads)
            meet(sp, "sp")

            def write_x(table, width):
                sp.wait_ge(s_norm, s_norm_n["sp"] + 1)
                s_norm_n["sp"] += 1
                store(sp, rows(table)[:, :, 0:D], xn[:])

            def sum_loads(m):
                def body(it):
                    for k in range(2):
                        c = chunk_of(sp, it, k)
                        sp.wait_ge(m["summed"], it * 2 + (k + 1))
                        sp.dma_start(idx[k], edge_slice(src, c)).then_inc(m["near"][k], 16)
                        sp.wait_ge(m["added"], it * 2 + (k + 1))
                        sp.dma_start(dst_i[k], edge_slice(dst, c, 1)).then_inc(m["far"][k], 16)
                steps(sp, body)
                meet(sp, "sp")

            write_x(x1_d, D)
            sp.wait_ge(s_out, stored[0])
            meet(sp, "sp")
            sum_loads(lin[0])

            write_x(x2_d, TW)
            sp.wait_ge(s_asd, 1)
            with nc.allow_non_contiguous_dma(reason="attention columns beside each node's features"):
                store(sp, rows(x2_d)[:, :, D:TW], asd[:, :, 0:H])
            sp.wait_ge(s_out, stored[0])
            meet(sp, "sp")

            def gat_max_loads(it):
                for k in range(2):
                    c = chunk_of(sp, it, k)
                    sp.wait_ge(g1["turned"], it * 8 + 4 * (k + 1))
                    sp.dma_start(idx[k], edge_slice(src, c)).then_inc(g1_a[k], 16)
                    sp.wait_ge(g1["added"], it * 2 + (k + 1))
                    sp.dma_start(dst_i[k], edge_slice(dst, c, 1)).then_inc(g1_b[k], 16)
                    sp.dma_start(next_i[k], edge_slice(dst, c, 2)).then_inc(g1_b[k], 16)
                    sp.dma_start(row4_i[k][:, 0:CHUNK + 1],
                                 dst[bass.ds(c * CHUNK, CHUNK + 1)].rearrange("(o e) -> o e", o=1)
                                 .partition_broadcast(H)).then_inc(g1_b[k], 16)
                for k in range(2):
                    c = chunk_of(sp, it, k)
                    sp.wait_ge(g1_g[k], (it + 1) * (16 * TILES))
                    sp.dma_start(edges_d[bass.ds(c * CHUNK, CHUNK), :].rearrange("(p t) f -> p t f", t=TILES),
                                 xa[k]).then_inc(g1_s[k], 16)
                    sp.wait_ge(g1_s[k], (it + 1) * 16)
                    hold(sp)
            steps(sp, gat_max_loads)
            meet(sp, "sp")

            sp.wait_ge(s_gat_tab, 1)
            store(sp, rows(gat_d), gat_n)
            sp.wait_ge(s_out, stored[0])
            meet(sp, "sp")

            def gat_sum_loads(it):
                for k in range(2):
                    c, b = chunk_of(sp, it, k), base_of(sp, it, k)
                    sp.wait_ge(g2["added"], it * 2 + (k + 1))
                    sp.dma_start(xa[k], edges_d[bass.ds(c * CHUNK, CHUNK), :]
                                 .rearrange("(p t) f -> p t f", t=TILES)).then_inc(g2_l[k], 16)
                    sp.dma_start(dst_i[k], edge_slice(dst, c, 1)).then_inc(g2_l[k], 16)
                    sp.dma_start(row2_i[k], dst[bass.ds(c * CHUNK + 1, CHUNK)].rearrange("(o e) -> o e", o=1)
                                 .partition_broadcast(WIN)).then_inc(g2_l[k], 16)
                    sp.dma_start(gat_win[k], gat_d[bass.ds(b, WIN), :]).then_inc(g2_l[k], 16)
            steps(sp, gat_sum_loads)
            meet(sp, "sp")

            write_x(x3_d, D)
            sp.wait_ge(s_out, stored[0])
            meet(sp, "sp")
            sum_loads(lin[1])
            sp.wait_ge(s_p, 1)
            store(sp, rows(p_d), p_n)
            sp.wait_ge(s_out, stored[0])
            meet(sp, "sp")
            sum_loads(lin[2])
            sp.wait_ge(s_norm, 4)
            whole = N // P
            store(sp, out[0:whole * P, :].rearrange("(b p) f -> p b f", p=P), xn[:, 0:whole, :])
            if N % P:
                store(sp, out[whole * P:N, :], xn[0:N % P, whole, :])
            sp.wait_ge(s_out, stored[0])
            meet(sp, "sp")

        @block.tensor
        def _(pe):
            meet(pe, "pe")
            pe_groups(0, len(FOURS), turn_to_features(D, lambda b: xn[:, b, :]))
            pe.wait_ge(s_evac[0], len(FOURS))

            def q_fill(g, b):
                for j in range(7):
                    n0 = (g * 7 + j) * P
                    m = pe.matmul(b[:, j * HID:(j + 1) * HID], acc[0:D, n0:n0 + P], w1_dst, start=True, stop=True)
                return m
            pe_groups(1, SEVENS, q_fill)
            meet(pe, "pe")

            pe.sem_inc(l0["xe_turned"], 8)
            pe.wait_ge(s_ready[0], 1)

            def mlp(it):
                for k in range(2):
                    pe.wait_ge(l0_g[k], (it + 1) * (16 * TILES))
                    hold(pe)
                    for j in range(4):
                        n = 4 * k + j
                        pe.wait_ge(l0["xe_t"], it * 8 + (n + 1))
                        hold(pe)
                        for t in range(4):
                            m = pe.transpose(bank[j % 2][0:2 * D, t * P:(t + 1) * P], xe[k][:, 4 * j + t, :], ident[:])
                        m.then_inc(l0["xe_turned"], 1)
                for k in range(2):
                    pe.wait_ge(l0["starts"], it * 2 + (k + 2))
                    pe.wait_ge(l0["xe_t"], it * 8 + (2 + 4 * (k + 1)))
                    hold(pe)
                    for j in range(5):
                        if j < 4:
                            n = 4 * k + j
                            e = slice(j * HALF, (j + 1) * HALF)
                            pe.wait_ge(l0["relu"], it * 8 + (n + 1))
                            hold(pe)
                            pe.matmul(bank[2 + j % 2][0:HID, :], w1_edge, xe_t[k][:, e], start=True, stop=False)
                            pe.matmul(bank[2 + j % 2][0:HID, :], q_win[k], onehot_t[k][:, e], start=False,
                                      stop=True).then_inc(l0["hidden"], 1)
                        if j >= 1:
                            n = 4 * k + j - 1
                            e = slice((j - 1) * HALF, j * HALF)
                            pe.wait_ge(l0["relu"], it * 8 + (2 + n + 1))
                            pe.wait_ge(l0["scanned"], it * 8 + (n + 1))
                            hold(pe)
                            pe.matmul(bank[4 + (j - 1) % 2][0:D, :], w2, hid_t[:, e], start=True,
                                      stop=True).then_inc(l0["values"], 1)
                for k in range(2):
                    pe.wait_ge(l0["scanned"], it * 8 + (2 + 4 * (k + 1)))
                    hold(pe)
                    r = run[k].rearrange("f (p t) -> f t p", t=TILES)
                    for t in range(TILES):
                        m = pe.transpose(bank[6][:, t * D:(t + 1) * D], r[:, t, :], ident[0:D, 0:D])
                    m.then_inc(l0["run_turned"], 1)
                    pe.wait_ge(l0["run_e"], it * 2 + (k + 1))
                    pe.wait_ge(l0["added"], it * 2 + (k + 2))
                    hold(pe)
                    for t in range(TILES):
                        m = pe.matmul(bank[7][0:D + 1, 0:WIN], run_e[:, t, :], onehot[k][:, t, :],
                                      start=(t == 0), stop=(t == TILES - 1))
                    m.then_inc(l0["picked"], 1)
            steps(pe, mlp)
            meet(pe, "pe")
            pe_groups(2, GROUPS, turn_to_nodes(D + 1, acc))
            meet(pe, "pe")

            def sums(n):
                m_ = lin[n]
                pe.sem_inc(m_["summed"], 2)
                pe.wait_ge(m_["ones"], 2)

                def body(it):
                    for k in range(2):
                        pe.wait_ge(m_["gathered"][k], (it + 1) * (16 * TILES))
                        pe.wait_ge(m_["onehot"], it * 2 + (k + 1))
                        pe.wait_ge(m_["added"], it * 2 + (k + 1))
                        hold(pe)
                        for t in range(TILES):
                            m = pe.matmul(bank[k][0:D + 1, 0:WIN], xg[k][:, t, :], onehot[k][:, t, :],
                                          start=(t == 0), stop=(t == TILES - 1))
                        m.then_inc(m_["summed"], 1)
                steps(pe, body)
                meet(pe, "pe")

            sums(0)
            pe_groups(3, GROUPS, turn_to_nodes(D + 1, acc))
            pe.wait_ge(s_norm, 2)
            for g, (b0, n) in enumerate(FOURS):
                if g >= 2:
                    pe.wait_ge(s_evac[4], g - 1)
                turn_to_features(D, lambda b: xn[:, b, :])(g, bank[g % 2]).then_inc(s_turn[4], 1)
            pe.wait_ge(s_evac[4], len(FOURS))
            for b in range(NB):
                m = pe.matmul(bank[2 + b // 49][:, (b % 49) * 2 * H:(b % 49 + 1) * 2 * H],
                              acc[0:D, b * P:(b + 1) * P], wa, start=True, stop=True)
            m.then_inc(s_terms, 1)
            meet(pe, "pe")

            pe.sem_inc(g1["turned"], 8)
            pe.wait_ge(s_ready[2], 1)

            def gat_max(it):
                for k in range(2):
                    pe.wait_ge(g1_g[k], (it + 1) * (16 * TILES))
                    hold(pe)
                    for j in range(4):
                        pe.wait_ge(g1["ad_t"], it * 8 + (4 * k + j + 1))
                        hold(pe)
                        for t in range(4):
                            m = pe.transpose(bank[j % 2][0:H, t * P:(t + 1) * P], xa[k][:, 4 * j + t, D:TW], ident[:])
                        m.then_inc(g1["turned"], 1)
                for k in range(2):
                    pe.wait_ge(g1["scanned"], it * 2 + (k + 1))
                    hold(pe)
                    r = run4[k].rearrange("f (p t) -> f t p", t=TILES)
                    for t in range(TILES):
                        m = pe.transpose(bank[6][:, t * H:(t + 1) * H], r[:, t, :], ident[0:H, 0:H])
                    m.then_inc(g1["run_turned"], 1)
                    pe.wait_ge(g1["run_e"], it * 2 + (k + 1))
                    pe.wait_ge(g1["added"], it * 2 + (k + 2))
                    hold(pe)
                    for t in range(TILES):
                        m = pe.matmul(bank[7][0:H, 0:WIN], run4_e[:, t, :], onehot[k][:, t, :],
                                      start=(t == 0), stop=(t == TILES - 1))
                    m.then_inc(g1["picked"], 1)
            steps(pe, gat_max)
            meet(pe, "pe")
            for b in range(NB):
                m = pe.transpose(bank[0][:, b * H:(b + 1) * H], acc[0:H, b * P:(b + 1) * P], ident[0:H, 0:H])
            m.then_inc(s_max_n, 1)
            meet(pe, "pe")

            pe.wait_ge(s_ready[3], 1)

            def gat_sum(it):
                for k in range(2):
                    pe.wait_ge(g2["onehots"], it * 2 + (k + 1))
                    hold(pe)
                    o = onehot2_t[k].rearrange("w (p t) -> w t p", t=TILES)
                    for t in range(TILES):
                        m = pe.matmul(bank[k][:, t * 2 * H:(t + 1) * 2 * H], o[:, t, :], gat_win[k],
                                      start=True, stop=True)
                    m.then_inc(g2["spread"], 1)
                for k in range(2):
                    pe.wait_ge(g2["msg"], it * 2 + (k + 1))
                    hold(pe)
                    for t in range(TILES):
                        pe.matmul(bank[2 + k][:, 0:WIN], msg[:, t, :], onehot[k][:, t, :],
                                  start=(t == 0), stop=(t == TILES - 1))
                    for t in range(TILES):
                        m = pe.matmul(bank[4 + k][0:H, 0:WIN], weight[k][:, t, :], onehot[k][:, t, :],
                                      start=(t == 0), stop=(t == TILES - 1))
                    m.then_inc(g2["summed"], 1)
            steps(pe, gat_sum)
            meet(pe, "pe")
            for b in range(NB):
                m = pe.transpose(bank[7][:, b * H:(b + 1) * H], den[0:H, b * P:(b + 1) * P], ident[0:H, 0:H])
            m.then_inc(s_max_n, 1)

            def heads_fill(g, b):
                b0, n = FOURS[g]
                for j in range(n):
                    m = pe.matmul(b[:, j * P:(j + 1) * P], acc[:, (b0 + j) * P:(b0 + j + 1) * P], w_heads,
                                  start=True, stop=True)
                return m
            pe_groups(5, len(FOURS), heads_fill)
            meet(pe, "pe")
            sums(1)
            pe_groups(6, GROUPS, turn_to_nodes(D + 1, acc))
            pe.wait_ge(s_cat, 1)
            pe_groups(7, len(FOURS), turn_to_features(2 * D, lambda b: cat_n[:, b, :]))
            pe.wait_ge(s_evac[7], len(FOURS))
            for g, (b0, n) in enumerate(FOURS):
                if g >= 2:
                    pe.wait_ge(s_hs, g - 1)
                pe.matmul(bank[2 + g % 2][0:HID, 0:n * P], s1, acc[0:2 * D, b0 * P:(b0 + n) * P],
                          start=True, stop=True).then_inc(s_hp, 1)
            pe.wait_ge(s_hs, len(FOURS))
            for g in range(SEVENS):
                if g >= 2:
                    pe.wait_ge(s_pr_out, g - 1)
                for j in range(7):
                    b = g * 7 + j
                    m = pe.matmul(bank[4 + g % 2][:, j * 2 * D:(j + 1) * 2 * D], hs_t[:, b * P:(b + 1) * P], s2,
                                  start=True, stop=True)
                m.then_inc(s_pr, 1)
            meet(pe, "pe")
            sums(2)
            for g in range(GROUPS):
                if g >= 2:
                    pe.wait_ge(s_fin_out, g - 1)
                turn_to_nodes(D + 1, acc)(g, bank[g % 2]).then_inc(s_fin, 1)
            meet(pe, "pe")

        @block.scalar
        def _(act):
            meet(act, "act")
            take_groups(act, 0, len(FOURS), empty_to(act_copy, acc, D))
            meet(act, "act")

            act.sem_inc(l0["xe_t"], 2)
            act.sem_inc(l0["relu"], 2)

            def mlp(it):
                for k in range(2):
                    act.wait_ge(l0_b[k], (it + 1) * 64)
                    act.wait_ge(l0["starts"], it * 2 + (k + 1))
                    act.activation(row_f[:, 0:CHUNK + 1], row_i[k][0:D, 0:CHUNK + 1], ACT.Copy,
                                   scale=-START).then_inc(l0["row_f"], 1)
                for k in range(2):
                    o = xe_t[k].rearrange("f (p t) -> f t p", t=TILES)
                    for j in range(4):
                        act.wait_ge(l0["xe_turned"], it * 8 + (8 + 4 * k + j + 1))
                        act.activation(o[:, 4 * j:4 * j + 4, :],
                                       bank[j % 2][0:2 * D, :].rearrange("f (t p) -> f t p", p=P),
                                       ACT.Copy).then_inc(l0["xe_t"], 1)
                for k in range(2):
                    for j in range(4):
                        act.wait_ge(l0["hidden"], it * 8 + (4 * k + j + 1))
                        act.activation(hid_t[:, j * HALF:(j + 1) * HALF], bank[2 + j % 2][0:HID, :], ACT.Relu,
                                       bias=b1_col).then_inc(l0["relu"], 1)
                for k in range(2):
                    act.wait_ge(l0["run_turned"], it * 2 + (k + 1))
                    act.activation(run_e[:, :, 0:D], bank[6][:, :].rearrange("p (t f) -> p t f", f=D),
                                   ACT.Copy).then_inc(l0["run_e"], 1)
            steps(act, mlp)
            meet(act, "act")

            def root():
                n = s_root[0] = s_root[0] + 1
                act.wait_ge(s_var, n)
                act.activation(rstd, var, ACT.Sqrt, bias=eps_col, scale=1.0 / D).then_inc(s_sqrt, 1)

            root()
            meet(act, "act")
            meet(act, "act")
            root()
            take_groups(act, 4, len(FOURS), empty_to(act_copy, acc, D))
            act.wait_ge(s_terms, 1)
            for h in range(2):
                act.activation(asd[:, 49 * h:49 * (h + 1), :],
                               bank[2 + h][:, 0:49 * 2 * H].rearrange("p (b f) -> p b f", f=2 * H),
                               ACT.Copy).then_inc(s_asd_half, 1)
            act.wait_ge(s_asd_half, 2)
            act.sem_inc(s_asd, 1)
            meet(act, "act")

            act.sem_inc(g1["ad_t"], 2)

            def gat_max(it):
                for k in range(2):
                    act.wait_ge(g1_b[k], (it + 1) * 48)
                    act.wait_ge(g1["starts"], it * 2 + (k + 1))
                    act.activation(row4_f[:, 0:CHUNK + 1], row4_i[k][:, 0:CHUNK + 1], ACT.Copy,
                                   scale=-START).then_inc(g1["row_f"], 1)
                for k in range(2):
                    o = ad_t[k].rearrange("f (p t) -> f t p", t=TILES)
                    for j in range(4):
                        act.wait_ge(g1["turned"], it * 8 + (8 + 4 * k + j + 1))
                        act.activation(o[:, 4 * j:4 * j + 4, :],
                                       bank[j % 2][0:H, :].rearrange("f (t p) -> f t p", p=P),
                                       ACT.Copy).then_inc(g1["ad_t"], 1)
                for k in range(2):
                    act.wait_ge(g1["run_turned"], it * 2 + (k + 1))
                    act.activation(run4_e, bank[6][:, 0:TILES * H].rearrange("p (t f) -> p t f", f=H),
                                   ACT.Copy).then_inc(g1["run_e"], 1)
            steps(act, gat_max)
            meet(act, "act")
            meet(act, "act")

            def gat_sum(it):
                for k in range(2):
                    act.wait_ge(g2["logit"], it * 2 + (k + 1))
                    act.activation(weight[k], logit[k], ACT.Exp).then_inc(g2["weight"], 1)
            steps(act, gat_sum)
            meet(act, "act")
            root()
            meet(act, "act")
            meet(act, "act")
            take_groups(act, 7, len(FOURS), empty_to(act_copy, acc, 2 * D))
            for g, (b0, n) in enumerate(FOURS):
                act.wait_ge(s_hp, g + 1)
                act.activation(hs_t[:, b0 * P:(b0 + n) * P], bank[2 + g % 2][0:HID, 0:n * P], ACT.Relu,
                               bias=sb1_col).then_inc(s_hs, 1)
            meet(act, "act")
            meet(act, "act")
            root()
            meet(act, "act")

        @block.vector
        def _(v):
            own = Own(v, "vector_own")
            v.wait_ge(s_plan_in, 32)
            own(v.tensor_copy(ends_f, ends_i))
            own(v.tensor_tensor(more_i, ends_f[:, 1, :], ends_f[:, 0, :], ALU.subtract))
            own(v.tensor_scalar(more_i, more_i, 5, None, ALU.arith_shift_right))
            own(v.tensor_scalar(more_i, more_i, 171.0, None, ALU.mult))
            own(v.tensor_scalar(more_i, more_i, 9, None, ALU.arith_shift_right))
            own(v.tensor_scalar(row_s, more_i, 1.0, None, ALU.add))
            own(v.memset(zero_s, 1.0))
            own(v.tensor_tensor_scan(val_s, zero_s, row_s, 0.0, ALU.mult, ALU.add))
            own(v.tensor_copy(count[0:1, 0:1], val_s[:, CH - 1:CH]))
            own(v.tensor_tensor(start_s[:, 0, :], val_s, row_s, ALU.subtract))
            own(v.scalar_tensor_tensor(out=val_s, in0=start_s[:, 0, :], scalar=-float(WIN), in1=ends_f[:, 0, :],
                                       op0=ALU.mult, op1=ALU.add))
            own(v.tensor_copy(start_s[:, 1, 0:1], val_s[:, 0:1]))
            own(v.tensor_tensor(start_s[:, 1, 1:CH], val_s[:, 1:CH], val_s[:, 0:CH - 1], ALU.subtract))
            v.sem_inc(s_plan_made, 1)
            v.wait_ge(s_plan_b, 1)
            v.wait_ge(s_step, 1)
            for j in range(TAB):
                s = step_s[:, j:j + 1]
                own(v.scalar_tensor_tensor(out=hit_s, in0=start_b[:, 0, :], scalar=s, in1=start_b[:, 0, :],
                                           op0=ALU.is_le, op1=ALU.bypass))
                own(v.tensor_reduce(got_s[:, 0, j:j + 1], hit_s, AX.X, ALU.add))
                own(v.tensor_tensor(hit_s, hit_s, start_b[:, 1, :], ALU.mult))
                own(v.tensor_reduce(got_s[:, 1, j:j + 1], hit_s, AX.X, ALU.add))
            own(v.tensor_scalar(got_s[:, 0, :], got_s[:, 0, :], -1.0, None, ALU.add))
            own(v.scalar_tensor_tensor(out=got_s[:, 1, :], in0=step_s, scalar=float(WIN), in1=got_s[:, 1, :],
                                       op0=ALU.mult, op1=ALU.add))
            own(v.tensor_scalar(got_s[:, 1, :], got_s[:, 1, :], float(NP), None, ALU.min))
            own(v.tensor_copy(got_i, got_s))
            v.sem_inc(s_plan_made, 1)
            v.wait_ge(s_plan_ld, 32)
            own(v.tensor_copy(base_f[:], base_i))
            v.wait_ge(s_in, 16 * 21)
            for half, o in ((1, 0), (0, H)):
                own(v.tensor_tensor(wprod, w_fho, fc_rows[:, half * D:(half + 1) * D]
                                    .rearrange("p (h o) -> p h o", h=1).to_broadcast([D, H, D]), ALU.mult))
                own(v.tensor_reduce(wa[:, o:o + H], wprod, AX.X, ALU.add))
            meet(v, "dve")

            v.memset(zero_tail, 0.0).then_inc(s_tail, 1)

            def q_out(g, b):
                return v.tensor_copy(q_n[:, 7 * g:7 * g + 7, :], b[:, 0:7 * HID].rearrange("p (b f) -> p b f", f=HID))
            take_groups(v, 1, SEVENS, q_out)
            meet(v, "dve")

            def window(it, k, chain, at_, ends):
                s = base_f[:, bass.ds(2 * it + k, 1)]
                v.tensor_scalar(win_f, iota_w[:], s, 1.0, ALU.add, ALU.add).then_inc(chain, 1)
                if ends:
                    v.tensor_tensor(last_f, dst_i[k], next_i[k], ALU.not_equal).then_inc(chain, 1)
                    v.wait_ge(chain, at_ + 2)
                    v.scalar_tensor_tensor(out=key_f, in0=dst_i[k], scalar=1.0, in1=last_f,
                                           op0=ALU.add, op1=ALU.mult).then_inc(chain, 1)
                    return at_ + 3
                v.tensor_scalar(key_f, dst_i[k], 1.0, None, ALU.add).then_inc(chain, 1)
                return at_ + 2

            def compare(k):
                return v.tensor_tensor(onehot[k], key_f.rearrange("p (t o) -> p t o", o=1).to_broadcast([P, TILES, WIN]),
                                       win_f.rearrange("p (o w) -> p o w", o=1).to_broadcast([P, TILES, WIN]),
                                       ALU.is_equal)

            v.memset(acc[0:D + 1, :], 0.0).then_inc(s_ready[0], 1)
            own(v.memset(run_e[:, :, D:D + 1], 1.0))
            own(v.memset(carry[:], START))
            v.wait_ge(s_ready[0], 1)
            v.sem_inc(l0["scanned"], 2)
            v.sem_inc(l0["starts"], 1)
            v.sem_inc(l0["added"], 2)

            def mlp(it):
                K = 26
                n = [0]
                base = it * K

                def link(ins):
                    n[0] += 1
                    ins.then_inc(l0["chain"], 1)
                    v.wait_ge(l0["chain"], base + n[0])

                for k in range(2):
                    v.wait_ge(l0_b[k], (it + 1) * 64)
                    n[0] = window_end = 7 * k
                    window(it, k, l0["chain"], base + n[0], True)
                    v.tensor_tensor(win_p[0:WIN, :], iota_p[0:WIN, :], base_f[0:WIN, bass.ds(2 * it + k, 1)],
                                    ALU.add).then_inc(l0["chain"], 1)
                    v.wait_ge(l0["chain"], base + (7 * k + 4))
                    compare(k).then_inc(l0["chain"], 1)
                    v.tensor_scalar(onehot_t[k], row_i[k][:, 1:CHUNK + 1], win_p[0:WIN, :], None,
                                    ALU.is_equal).then_inc(l0["chain"], 1)
                    v.wait_ge(l0["row_f"], it * 2 + (k + 1))
                    v.wait_ge(l0["chain"], base + (7 * k + 6))
                    v.tensor_tensor(starts[k], row_f[:, 0:CHUNK], row_f[:, 1:CHUNK + 1],
                                    ALU.subtract).then_inc(l0["starts"], 1)
                    v.sem_inc(l0["chain"], 1)
                n[0] = 14
                for k in range(2):
                    c = chunk_of(v, it, k)
                    v.wait_ge(l0["starts"], it * 2 + (k + 2))
                    link(v.tensor_copy(first, carry[:, bass.ds(c, 1)]))
                    for j in range(4):
                        v.wait_ge(l0["values"], it * 8 + (4 * k + j + 1))
                        e = slice(j * HALF, (j + 1) * HALF)
                        v.tensor_tensor_scan(run[k][:, e], starts[k][:, e], bank[4 + j % 2][0:D, :],
                                             first if j == 0 else run[k][:, j * HALF - 1:j * HALF],
                                             ALU.add, ALU.max).then_inc(l0["scanned"], 1)
                        v.wait_ge(l0["scanned"], it * 8 + (2 + 4 * k + j + 1))
                    link(v.tensor_copy(carry[:, bass.ds(c + 1, 1)], run[k][:, CHUNK - 1:CHUNK]))
                for k in range(2):
                    b = base_of(v, it, k)
                    v.wait_ge(l0["picked"], it * 2 + (k + 1))
                    v.tensor_tensor(acc[0:D + 1, bass.ds(b, WIN)], acc[0:D + 1, bass.ds(b, WIN)],
                                    bank[7][0:D + 1, 0:WIN], ALU.add).then_inc(l0["added"], 1)
                    v.wait_ge(l0["added"], it * 2 + (2 + k + 1))
                    hold(v)
                v.sem_inc(l0["chain"], K - n[0])
            steps(v, mlp)
            meet(v, "dve")

            def wide(row, f=D):
                return row.rearrange("p (b o) -> p b o", o=1).to_broadcast([P, NB, f])

            def beside(row, f=D):
                return row.rearrange("p (o f) -> p o f", o=1).to_broadcast([P, NB, f])

            def layer_norm(y):
                own(v.tensor_reduce(mean, y, AX.X, ALU.add))
                own(v.tensor_scalar(mean, mean, 1.0 / D, None, ALU.mult))
                own(v.tensor_tensor(cen, y, wide(mean), ALU.subtract))
                own(v.tensor_tensor(sq, cen, cen, ALU.mult))
                v.tensor_reduce(var, sq, AX.X, ALU.add).then_inc(s_var, 1)
                s_dve_root[0] += 1
                v.wait_ge(s_sqrt, s_dve_root[0])
                own(v.reciprocal(rstd, rstd))
                v.tensor_tensor(xn[:], cen, wide(rstd), ALU.mult).then_inc(s_norm, 1)

            def take_nodes(turned, evac, width, scale=None):
                for g in range(GROUPS):
                    v.wait_ge(turned, g + 1)
                    of = bank[g % 2][:, 0:GROUP * width].rearrange("p (b f) -> p b f", f=width)
                    to = yn[:, g * GROUP:(g + 1) * GROUP, 0:width]
                    if scale is None:
                        v.tensor_copy(to, of).then_inc(evac, 1)
                    else:
                        r = scale[:, g * GROUP:(g + 1) * GROUP]
                        v.tensor_tensor(to, of, r.rearrange("p (b o) -> p b o", o=1)
                                        .to_broadcast([P, GROUP, width]), ALU.mult).then_inc(evac, 1)
                v.wait_ge(evac, GROUPS)

            take_nodes(s_turn[2], s_evac[2], D + 1)
            y = yn[:, :, 0:D]
            own(v.tensor_scalar(has, yn[:, :, D:D + 1].rearrange("p b o -> p (b o)"), -1.0, EMPTY, ALU.add, ALU.mult))
            own(v.tensor_tensor(y, y, beside(b2_row), ALU.add))
            own(v.tensor_tensor(y, y, wide(has), ALU.add))
            own(v.tensor_tensor(y, y, xn[:], ALU.max))
            own(v.tensor_tensor(y, y, xn[:], ALU.add))
            layer_norm(y)
            meet(v, "dve")

            def sums(n):
                m_ = lin[n]
                v.memset(acc[0:D + 1, :], 0.0).then_inc(m_["chain"], 1)
                for k in range(2):
                    v.memset(xg[k][:, :, D:D + 1], 1.0).then_inc(m_["ones"], 1)
                v.wait_ge(m_["chain"], 1)
                v.sem_inc(m_["added"], 2)

                def body(it):
                    for k in range(2):
                        v.wait_ge(m_["far"][k], (it + 1) * 16)
                        window(it, k, m_["chain"], it * 4 + (1 + 2 * k), False)
                        v.wait_ge(m_["chain"], it * 4 + (1 + 2 * k + 2))
                        compare(k).then_inc(m_["onehot"], 1)
                        v.wait_ge(m_["onehot"], it * 2 + (k + 1))
                    for k in range(2):
                        b = base_of(v, it, k)
                        v.wait_ge(m_["summed"], it * 2 + (2 + k + 1))
                        v.tensor_tensor(acc[0:D + 1, bass.ds(b, WIN)], acc[0:D + 1, bass.ds(b, WIN)],
                                        bank[k][0:D + 1, 0:WIN], ALU.add).then_inc(m_["added"], 1)
                        v.wait_ge(m_["added"], it * 2 + (2 + k + 1))
                    hold(v)
                steps(v, body)
                meet(v, "dve")

            sums(0)
            take_nodes(s_turn[3], s_evac[3], D + 1)
            own(v.tensor_scalar(rdeg[:], yn[:, :, D:D + 1].rearrange("p b o -> p (b o)"), 1.0, None, ALU.max))
            own(v.reciprocal(rdeg[:], rdeg[:]))
            own(v.tensor_tensor(y, y, xn[:], ALU.add))
            layer_norm(y)
            meet(v, "dve")

            v.memset(acc[:], 0.0).then_inc(s_ready[2], 1)
            own(v.memset(carry[:], START))
            v.wait_ge(s_ready[2], 1)
            v.sem_inc(g1["added"], 2)
            v.sem_inc(g1["starts"], 1)

            def gat_max(it):
                K = 14
                base = it * K
                for k in range(2):
                    v.wait_ge(g1_b[k], (it + 1) * 48)
                    window(it, k, g1["chain"], base + 5 * k, True)
                    v.wait_ge(g1["chain"], base + (5 * k + 3))
                    compare(k).then_inc(g1["chain"], 1)
                    v.wait_ge(g1["row_f"], it * 2 + (k + 1))
                    v.wait_ge(g1["chain"], base + (5 * k + 4))
                    v.tensor_tensor(starts4[k], row4_f[:, 0:CHUNK], row4_f[:, 1:CHUNK + 1],
                                    ALU.subtract).then_inc(g1["starts"], 1)
                    v.sem_inc(g1["chain"], 1)
                for k in range(2):
                    c = chunk_of(v, it, k)
                    v.wait_ge(g1["starts"], it * 2 + (k + 2))
                    v.tensor_copy(first4, carry[0:H, bass.ds(c, 1)]).then_inc(g1["chain"], 1)
                    v.wait_ge(g1["chain"], base + (10 + 2 * k + 1))
                    v.wait_ge(g1["ad_t"], it * 8 + (2 + 4 * (k + 1)))
                    v.tensor_tensor_scan(run4[k], starts4[k], ad_t[k], first4, ALU.add,
                                         ALU.max).then_inc(g1["scanned"], 1)
                    v.wait_ge(g1["scanned"], it * 2 + (k + 1))
                    v.tensor_copy(carry[0:H, bass.ds(c + 1, 1)], run4[k][:, CHUNK - 1:CHUNK]).then_inc(g1["chain"], 1)
                    v.wait_ge(g1["chain"], base + (10 + 2 * k + 2))
                for k in range(2):
                    b = base_of(v, it, k)
                    v.wait_ge(g1["picked"], it * 2 + (k + 1))
                    v.tensor_tensor(acc[0:H, bass.ds(b, WIN)], acc[0:H, bass.ds(b, WIN)],
                                    bank[7][0:H, 0:WIN], ALU.add).then_inc(g1["added"], 1)
                    v.wait_ge(g1["added"], it * 2 + (2 + k + 1))
                    hold(v)
            steps(v, gat_max)
            meet(v, "dve")

            v.wait_ge(s_max_n, 1)
            own(v.tensor_scalar(gat_n[:, :, 0:H], asd[:, :, H:2 * H], fc_b_col, None, ALU.add))
            own(v.tensor_tensor(gat_n[:, :, H:2 * H], gat_n[:, :, 0:H],
                                bank[0][:, 0:NB * H].rearrange("p (b f) -> p b f", f=H), ALU.add))
            own(v.tensor_scalar(gat_u, gat_n[:, :, H:2 * H], 0.2, None, ALU.mult))
            own(v.tensor_tensor(gat_n[:, :, H:2 * H], gat_n[:, :, H:2 * H], gat_u, ALU.max))
            v.sem_inc(s_gat_tab, 1)
            meet(v, "dve")

            v.memset(acc[:], 0.0).then_inc(s_ready[3], 1)
            own(v.memset(den, 0.0))
            v.wait_ge(s_ready[3], 1)
            v.sem_inc(g2["added"], 2)

            def gat_sum(it):
                K = 24
                base = it * K
                n = [0]

                def link(ins):
                    n[0] += 1
                    ins.then_inc(g2["chain"], 1)
                    v.wait_ge(g2["chain"], base + n[0])

                for k in range(2):
                    v.wait_ge(g2_l[k], (it + 1) * 64)
                    n[0] = window_at = 4 * k
                    window(it, k, g2["chain"], base + n[0], False)
                    n[0] += 2
                    link(v.tensor_tensor(win_p[0:WIN, :], iota_p[0:WIN, :],
                                         base_f[0:WIN, bass.ds(2 * it + k, 1)], ALU.add))
                    link(compare(k))
                    v.tensor_scalar(onehot2_t[k], row2_i[k], win_p[0:WIN, :], None,
                                    ALU.is_equal).then_inc(g2["onehots"], 1)
                    v.wait_ge(g2["onehots"], it * 2 + (k + 1))
                for k in range(2):
                    v.wait_ge(g2["spread"], it * 2 + (k + 1))
                    of = bank[k][:, 0:TILES * 2 * H].rearrange("p (t f) -> p t f", f=2 * H)
                    link(v.tensor_tensor(logit[k], xa[k][:, :, D:TW], of[:, :, 0:H], ALU.add))
                    link(v.tensor_scalar(tmp4, logit[k], 0.2, None, ALU.mult))
                    link(v.tensor_tensor(logit[k], logit[k], tmp4, ALU.max))
                    v.tensor_tensor(logit[k], logit[k], of[:, :, H:2 * H], ALU.subtract).then_inc(g2["logit"], 1)
                for k in range(2):
                    b = base_of(v, it, k)
                    v.wait_ge(g2["weight"], it * 2 + (k + 1))
                    for h in range(H):
                        m = v.tensor_tensor(msg[:, :, h * D:(h + 1) * D], xa[k][:, :, 0:D],
                                            weight[k][:, :, h:h + 1].to_broadcast([P, TILES, D]), ALU.mult)
                        if h == H - 1:
                            m.then_inc(g2["msg"], 1)
                        else:
                            link(m)
                    v.wait_ge(g2["summed"], it * 2 + (k + 1))
                    link(v.tensor_tensor(den[:, bass.ds(b, WIN)], den[:, bass.ds(b, WIN)],
                                         bank[4 + k][0:H, 0:WIN], ALU.add))
                    v.tensor_tensor(acc[:, bass.ds(b, WIN)], acc[:, bass.ds(b, WIN)],
                                    bank[2 + k][:, 0:WIN], ALU.add).then_inc(g2["added"], 1)
                    v.wait_ge(g2["added"], it * 2 + (2 + k + 1))
                    hold(v)
                v.sem_inc(g2["chain"], K - n[0])
            steps(v, gat_sum)
            meet(v, "dve")

            v.wait_ge(s_max_n, 2)
            own(v.tensor_scalar(gat_u, bank[7][:, 0:NB * H].rearrange("p (b f) -> p b f", f=H), 1e-30, None, ALU.max))
            own(v.reciprocal(gat_u, gat_u))
            own(v.tensor_scalar(gat_u, gat_u, 1.0 / H, None, ALU.mult))
            for g, (b0, n) in enumerate(FOURS):
                v.wait_ge(s_turn[5], g + 1)
                t4 = heads_tmp[g % 2][:, 0:n * P]
                v.tensor_tensor(t4.rearrange("p (a o) -> p a o", o=D),
                                bank[g % 2][:, 0:n * P].rearrange("p (a o) -> p a o", o=D),
                                gat_u[:, b0:b0 + n, :].rearrange("p b (h o) -> p (b h) o", o=1)
                                .to_broadcast([P, n * H, D]), ALU.mult).then_inc(s_evac[5], 1)
                v.wait_ge(s_evac[5], g + 1)
                own(v.tensor_reduce(yn[:, b0:b0 + n, 0:D], t4.rearrange("p (b h o) -> p b o h", h=H, o=D),
                                    AX.X, ALU.add))
            own(v.tensor_tensor(y, y, beside(gat_bias_row), ALU.add))
            own(v.tensor_tensor(y, y, xn[:], ALU.add))
            layer_norm(y)
            meet(v, "dve")

            sums(1)
            take_nodes(s_turn[6], s_evac[6], D + 1, rdeg)
            own(v.tensor_copy(cat_n[:, :, 0:D], y))
            v.tensor_copy(cat_n[:, :, D:2 * D], xn[:]).then_inc(s_cat, 1)
            for g in range(SEVENS):
                v.wait_ge(s_pr, g + 1)
                of = bank[4 + g % 2][:, 0:7 * 2 * D].rearrange("p (b f) -> p b f", f=2 * D)
                own(v.tensor_copy(p_n[:, 7 * g:7 * g + 7, :], of[:, :, 0:D]))
                v.tensor_copy(res_n[:, 7 * g:7 * g + 7, :], of[:, :, D:2 * D]).then_inc(s_pr_out, 1)
            v.wait_ge(s_pr_out, SEVENS)
            v.sem_inc(s_p, 1)
            own(v.tensor_tensor(res_n, res_n, beside(sb2_row), ALU.add))
            own(v.tensor_tensor(xn[:], res_n, xn[:], ALU.add))
            meet(v, "dve")
            sums(2)
            take_nodes(s_fin, s_fin_out, D + 1, rdeg)
            own(v.tensor_tensor(y, y, xn[:], ALU.add))
            layer_norm(y)
            meet(v, "dve")



_OUT = (12500, 32)


def kernel(**inputs):
    import numpy as np
    import concourse.bacc as bacc
    from concourse.bass_utils import run_bass_kernel_spmd

    n, e = _OUT[0], inputs["src"].shape[0]
    chunks, _ = sizes(n, e)
    pad_n = -(-n // P) * P - n
    pad_e = chunks * CHUNK - e
    arrays = {
        "x": np.pad(np.asarray(inputs["x"]), ((0, pad_n), (0, 0))),
        "src": np.pad(np.asarray(inputs["src"]), (0, pad_e)),
        "dst": np.concatenate([np.full(1, -1, np.int32), np.asarray(inputs["dst"]), np.full(pad_e, n, np.int32),
                               np.full(1, n, np.int32)]),
        "edge_attr": np.pad(np.asarray(inputs["edge_attr_32"]), ((0, pad_e), (0, 0))),
    }
    for name in ("L0_gnn_W1", "L0_gnn_b1", "L0_gnn_W2", "L0_gnn_b2", "L2_gnn_w", "L2_gnn_fc_w", "L2_gnn_fc_b",
                 "L2_gnn_bias", "L3_gnn_W1_l", "L3_gnn_b1", "L3_gnn_W1_r", "L3_gnn_W2_l", "L3_gnn_b2", "L3_gnn_W2_r"):
        arrays[name] = np.ascontiguousarray(inputs[name])
    nc = bacc.Bacc("TRN2", target_bir_lowering=False, num_devices=1)
    args = [nc.dram_tensor(k, v.shape, mybir.dt.from_np(v.dtype), kind="ExternalInput").ap() for k, v in arrays.items()]
    out = nc.dram_tensor("out", _OUT, F32, kind="ExternalOutput").ap()
    gnn(nc, *args, out, e)
    r = run_bass_kernel_spmd(nc, [arrays], core_ids=[0])
    return r.results[0]["out"]
```

```python
from contextlib import ExitStack

import concourse.bass as bass
from concourse import mybir

ALU = mybir.AluOpType
ACT = mybir.ActivationFunctionType
AX = mybir.AxisListType
F32 = mybir.dt.float32
I32 = mybir.dt.int32
BF16 = mybir.dt.bfloat16

P = 128
TILES = 8
CHUNK = P * TILES
WIN = 48
SLOTS = 4
SLICE = 512
EPS = 1e-5
START = -(2.0 ** 100)
EMPTY = 1e30


def sizes(n_nodes, n_edges):
    chunks = -(-n_edges // CHUNK)
    chunks += -chunks % SLOTS
    steps = chunks + n_nodes // WIN + 1
    return chunks, steps + -steps % SLOTS


def gnn(nc, x, src, dst, edge_attr, W1, b1, W2, b2, gat_w, fc_w, fc_b, gat_bias,
        S1l, sb1, S1r, S2l, sb2, S2r, out, n_edges):
    N, D = out.shape
    NP = x.shape[0]
    NB = NP // P
    NT = NP + P
    HID = W1.shape[1]
    H = gat_w.shape[0]
    CH, STEPS = sizes(N, n_edges)
    TAB = -(-STEPS // P)
    TW = D + H
    NS = CHUNK // SLICE
    TS = TILES // NS
    assert D == 32 and HID == 64 and H * D == P and NP % P == 0

    with ExitStack() as ctx:
        def sb(name, shape, dt=F32):
            return ctx.enter_context(nc.sbuf_tensor(name, shape, dt))

        def sem(name):
            return ctx.enter_context(nc.semaphore(name))

        def slots(name):
            return [sem(f"{name}{k}") for k in range(SLOTS)]

        def dram(name, shape, dt=F32):
            return nc.dram_tensor(name, shape, dt, kind="Internal").ap()

        plan_d = dram("plan_d", (2, TAB * P), I32)
        count_d = dram("count_d", (1, 1), I32)
        q_d = dram("q_d", (NT, HID))
        x1_d = dram("x1_d", (NP, D))
        x2_d = dram("x2_d", (NP, TW))
        gat_d = dram("gat_d", (NT, 3 * 2 * H), BF16)
        edges_d = dram("edges_d", (STEPS * CHUNK, TW))
        prime_d = dram("prime_d", (SLOTS, D))
        x3_d = dram("x3_d", (NP, D))
        p_d = dram("p_d", (NP, D))

        acc = sb("acc", [P, NT])
        xn = sb("xn", [P, NB, D])
        rdeg = sb("rdeg", [P, NB])
        ident = sb("ident", [P, P])
        iota_w = sb("iota_w", [P, WIN])
        iota_p = sb("iota_p", [P, 1])
        base_f = sb("base_f", [P, TAB * P])
        plan = sb("plan", [1, 2, TAB * P], I32)
        count = sb("count", [1, 1], I32)
        base_late = sb("base_late", [1, SLOTS + TAB * P], I32)
        small = sb("small", [P, 640])
        carry = sb("carry", [D, CH + 1])
        WORK = 31100
        work = sb("work", [P, WORK])
        yn = work[:, WORK - NB * TW:WORK].rearrange("p (b f) -> p b f", f=TW)

        class Arena:
            def __init__(self):
                self.at = 0

            def __call__(self, parts, *dims, dt=F32):
                n = 1
                for d in dims:
                    n *= d
                v = work[0:parts, self.at:self.at + n]
                self.at += n + n % 2
                assert self.at <= WORK, self.at
                if dt is not F32:
                    v = v.bitcast(dt)
                if len(dims) == 2:
                    v = v.rearrange("p (a b) -> p a b", a=dims[0])
                return v

        bank = [ctx.enter_context(nc.psum_tensor(f"bank{i}", [P, 512], F32)) for i in range(8)]

        at = [0]

        def param(parts, n):
            v = small[0:parts, at[0]:at[0] + n]
            at[0] += n
            assert at[0] <= 640
            return v

        w1_edge = param(2 * D, HID)
        w1_dst = param(D, HID)
        w2 = param(HID, D)
        b1_col = param(HID, 1)
        b2_row = param(P, D)
        wa = param(D, 2 * H)
        fc_b_col = param(P, 1)
        gat_bias_row = param(P, D)
        w_heads = param(P, P)
        s1 = param(2 * D, HID)
        sb1_col = param(HID, 1)
        s2 = param(HID, 2 * D)
        sb2_row = param(P, D)
        eps_col = param(P, 1)
        one_col = param(P, 1)

        block = ctx.enter_context(nc.Block())

        arrived = sem("arrived")
        meetings = {}

        def meet(eng, who):
            meetings[who] = meetings.get(who, 0) + 1
            eng.drain().then_inc(arrived, 1)
            eng.wait_ge(arrived, 5 * meetings[who])

        held = sem("held")

        def hold(eng):
            eng.sem_inc(held, 1)

        def steps(eng, body):
            n = eng.value_load(count[0:1, 0:1], min_val=CH, max_val=STEPS)
            with eng.Fori(0, CH // SLOTS) as it:
                body(it)
            with eng.If(n > CH):
                with eng.Fori(CH // SLOTS, STEPS // SLOTS) as it:
                    with eng.If(n > SLOTS * it):
                        body(it)
            return n

        def chunk_of(eng, it, k):
            return eng.value_load(plan[0:1, 0, bass.ds(SLOTS * it + k, 1)], min_val=0, max_val=CH - 1)

        def base_of(eng, it, k):
            return eng.value_load(plan[0:1, 1, bass.ds(SLOTS * it + k, 1)], min_val=0, max_val=NP)

        def edge_slice(flat, c, first=0):
            return flat[bass.ds(c * CHUNK + first, CHUNK)].rearrange("(p t) -> p t", t=TILES)

        def rows(table):
            return table[0:NP, :].rearrange("(b p) f -> p b f", p=P)

        GROUP = 14
        GROUPS = NB // GROUP
        FOURS = [(b, min(4, NB - b)) for b in range(0, NB, 4)]
        SEVENS = NB // 7
        assert NB % GROUP == 0

        class Own:

            def __init__(self, eng, name, per=0, it=None):
                self.eng, self.s, self.n = eng, sem(name), 0

            def __call__(self, ins):
                self.n += 1
                ins.then_inc(self.s, 1)
                self.eng.wait_ge(self.s, self.n)

        s_in = sem("inputs_loaded")
        s_const = sem("constants_made")
        s_zero = sem("heads_zeroed")
        s_wa = sem("attention_rows_made")
        s_plan_in, s_plan_made = sem("plan_loaded"), sem("plan_made")
        s_plan_b = sem("plan_broadcast")
        s_plan_st, s_plan_ld = sem("plan_stored"), sem("plan_reloaded")
        names = "abcdefgh"
        s_turn = [sem(f"turned_{c}") for c in names]
        s_evac = [sem(f"evacuated_{c}") for c in names]
        s_turn_n, s_evac_n = {}, {}
        s_out = sem("stored")
        stored = [0]

        def store(eng, to, of):
            eng.dma_start(to, of).then_inc(s_out, 16)
            stored[0] += 16

        def pe_groups(i, n, fill):
            for g in range(n):
                if g >= 2:
                    nc.tensor.wait_ge(s_evac[i], g - 1)
                fill(g, bank[g % 2]).then_inc(s_turn[i], 1)

        def take_groups(eng, i, n, empty):
            for g in range(n):
                eng.wait_ge(s_turn[i], g + 1)
                empty(g, bank[g % 2]).then_inc(s_evac[i], 1)

        def turn_to_nodes(parts, of):
            def fill(g, b):
                for j in range(GROUP):
                    n0 = (g * GROUP + j) * P
                    m = nc.tensor.transpose(b[:, j * parts:(j + 1) * parts], of[0:parts, n0:n0 + P],
                                            ident[0:parts, 0:parts])
                return m
            return fill

        def turn_to_features(width, of):
            def fill(g, b):
                b0, n = FOURS[g]
                for j in range(n):
                    m = nc.tensor.transpose(b[0:width, j * P:(j + 1) * P], of(b0 + j), ident[:, :])
                return m
            return fill

        def empty_to(eng_copy, to, width):
            def empty(g, b):
                b0, n = FOURS[g]
                return eng_copy(to[0:width, b0 * P:(b0 + n) * P], b[0:width, 0:n * P])
            return empty

        act_copy = lambda o, i: nc.scalar.activation(o, i, ACT.Copy)

        a = Arena()
        xe = [a(P, TILES, 2 * D) for _ in range(SLOTS)]
        idx = [a(P, TILES, dt=I32) for _ in range(SLOTS)]
        dst_i = [a(P, TILES, dt=I32) for _ in range(SLOTS)]
        next_i = [a(P, TILES, dt=I32) for _ in range(SLOTS)]
        last_f = a(P, TILES)
        key_f = a(P, TILES)
        win_f = a(P, WIN)
        win_p = a(P, 1)
        onehot = [a(P, TILES, WIN) for _ in range(SLOTS)]
        LIN = a.at
        W0 = 2 * D
        W1_ = W0 + WIN
        row_i = [a(P, CHUNK + 2, dt=I32) for _ in range(SLOTS)]
        xo_t = [a(W1_, CHUNK) for _ in range(SLOTS)]
        w_step = [a(W1_, HID) for _ in range(SLOTS)]
        row_f = a(D, CHUNK + 2)
        starts = [a(D, CHUNK) for _ in range(SLOTS)]
        hid_t = [a(HID, SLICE) for _ in range(2)]
        run = [a(D, CHUNK) for _ in range(SLOTS)]
        first = a(D, 1)
        run_e = [a(P, TILES, D + 1) for _ in range(2)]

        l0 = {n: sem("mlp_" + n) for n in (
            "xe_turned", "xe_t", "hidden", "relu", "values", "scanned", "run_turned", "run_e",
            "picked", "added", "weights", "starts", "row_f", "chain")}
        l0_a, l0_b, l0_g = slots("mlp_near_loaded"), slots("mlp_far_loaded"), slots("mlp_gathered")

        a = Arena()
        a.at = LIN
        xg = [a(P, TILES, D + 1) for _ in range(SLOTS)]

        a = Arena()
        a.at = LIN
        xa = [a(P, TILES, TW) for _ in range(SLOTS)]
        row4_i = [a(H, CHUNK + 2, dt=I32) for _ in range(SLOTS)]
        row4_f = a(H, CHUNK + 2)
        starts4 = [a(H, CHUNK) for _ in range(SLOTS)]
        ad_t = [a(H, CHUNK) for _ in range(SLOTS)]
        run4 = [a(H, CHUNK) for _ in range(SLOTS)]
        first4 = a(H, 1)
        run4_e = [a(P, TILES, H) for _ in range(2)]
        a = Arena()
        a.at = LIN
        a(P, SLOTS * TILES * TW)
        row2_i = [a(WIN, CHUNK, dt=I32) for _ in range(SLOTS)]
        far_f = a(WIN, CHUNK)
        own_f = a(WIN, 1)
        onehot2_t = [a(WIN, CHUNK // 2).bitcast(BF16) for _ in range(SLOTS)]
        gat_win = [a(WIN, 3 * H).bitcast(BF16) for _ in range(SLOTS)]
        near_f = [a(P, TILES, 2 * H) for _ in range(2)]
        logit = [a(P, TILES, H) for _ in range(SLOTS)]
        msg = [a(P, TILES, P + H) for _ in range(SLOTS)]
        sum_n = [a(WIN, P + H) for _ in range(2)]
        den = a(H, NT)

        def gathers(g, name, table, to, width, ready, ready_n, done):
            def body(it):
                for k in range(SLOTS):
                    g.wait_ge(ready[k], (it + 1) * (16 * ready_n))
                    hold(g)
                    for t in range(TILES):
                        g.indirect_dma_start(
                            to[k][:, t, 0:width], None, table,
                            bass.IndirectOffsetOnAxis(idx[k][:, t:t + 1], 0)).then_inc(done[k], 16)
            steps(g, body)

        spread_bank = [bank[1], bank[6], bank[7], bank[0]]
        assert SLOTS == 4
        lin = []
        for n in range(3):
            lin.append(dict(
                loaded=slots(f"sum{n}_loaded"),
                gathered=slots(f"sum{n}_gathered"), onehot=sem(f"sum{n}_onehot"),
                summed=sem(f"sum{n}_summed"), added=sem(f"sum{n}_added"),
                chain=sem(f"sum{n}_chain"), ones=sem(f"sum{n}_ones")))
        g1 = {n: sem("gat_max_" + n) for n in (
            "turned", "ad_t", "row_f", "starts", "scanned", "run_turned", "run_e", "picked", "added",
            "chain")}
        g1_a, g1_b, g1_g, g1_s = (slots("gat_max_idx_loaded"), slots("gat_max_dst_loaded"),
                                  slots("gat_max_gathered"), slots("gat_max_stored"))
        g2 = {n: sem("gat_sum_" + n) for n in (
            "onehot_t", "spread", "logit", "weight", "msg", "summed", "sum_n", "turned", "added", "chain", "row")}
        g2_l = slots("gat_sum_dst_loaded")
        g2_x = g1_g

        a = Arena()
        ends_i = a(1, 2, CH, dt=I32)
        more_i = a(1, CH, dt=I32)
        row_s = a(1, CH)
        zero_s = a(1, CH)
        start_s = a(1, 2, CH)
        val_s = a(1, CH)
        start_b = a(P, 2, CH)
        step_s = a(P, TAB)
        hit_s = a(P, CH)
        got_s = a(P, 2, TAB)
        got_i = a(P, 2, TAB, dt=I32)
        n_i = a(1, 1, dt=I32)
        ends_f = a(1, 2, CH)
        s_step = sem("step_numbers")

        def plan_gpsimd(g):
            g.iota(step_s, [[P, TAB]], base=0, channel_multiplier=1,
                   allow_small_or_imprecise_dtypes=True).then_inc(s_step, 1)
            g.wait_ge(s_plan_made, 1)
            g.partition_broadcast(start_b.rearrange("p a b -> p (a b)"),
                                  start_s.rearrange("p a b -> p (a b)")).then_inc(s_plan_b, 1)

        fc_rows = work[0:D, 8000:8000 + 2 * D]
        w_fho = work[0:D, 8100:8100 + P].rearrange("p (h o) -> p h o", h=H)
        wprod = work[0:D, 8300:8300 + P].rearrange("p (h o) -> p h o", h=H)
        base_i = work[:, 9000:9000 + TAB * P].bitcast(I32)
        q_n = work[:, 0:NB * HID].rearrange("p (b f) -> p b f", f=HID)
        zero_tail = work[:, NB * HID:NB * HID + HID]
        cen = work[:, 0:NB * D].rearrange("p (b f) -> p b f", f=D)
        sq = work[:, NB * D:2 * NB * D].rearrange("p (b f) -> p b f", f=D)
        mean = work[:, 2 * NB * D:2 * NB * D + NB]
        var = work[:, 2 * NB * D + NB:2 * NB * D + 2 * NB]
        rstd = work[:, 2 * NB * D + 2 * NB:2 * NB * D + 3 * NB]
        has = work[:, 2 * NB * D + 3 * NB:2 * NB * D + 4 * NB]
        MORE = 2 * NB * D + 4 * NB
        res_n = work[:, MORE:MORE + NB * D].rearrange("p (b f) -> p b f", f=D)
        hs_t = work[0:HID, MORE + NB * D:MORE + NB * D + NP]
        asd = sb("asd", [P, NB, 2 * H])
        gat_n = work[:, 0:NB * 2 * H].rearrange("p (b f) -> p b f", f=2 * H)
        gat_parts = work[:, 2000:2000 + NB * 3 * H].bitcast(BF16).rearrange("p (b q f) -> p b q f", q=3, f=2 * H)
        gat_u = work[:, 1000:1000 + NB * H].rearrange("p (b f) -> p b f", f=H)
        p_n = cen
        s_tail = sem("zero_tail")
        s_norm = sem("normed")
        s_norm_n = {"sp": 0}
        s_asd = sem("attention_terms")
        s_gat_tab = sem("attention_table")
        s_p = sem("projected")
        s_ready = {i: sem(f"acc_zero{i}") for i in (0, 2, 3)}

        s_terms, s_max_n, s_cat, s_hp, s_hs = (sem(n) for n in ("terms", "max_turned", "cat", "hid_made", "hid_relu"))
        s_pr, s_pr_out, s_fin, s_fin_out = (sem(n) for n in ("projections", "projections_out", "fin_turned", "fin_out"))
        s_sqrt = sem("sqrt")
        s_var = sem("variance")
        cat_n = work[:, 0:NB * 2 * D].rearrange("p (b f) -> p b f", f=2 * D)

        s_root = [0]
        s_asd_half = sem("attention_terms_half")

        s_dve_root = [0]
        heads_tmp = [work[:, MORE + 512 * i:MORE + 512 * (i + 1)] for i in range(2)]

        @block.gpsimd
        def _(g):
            g.memset(ident[:], 0.0).then_inc(s_const, 1)
            g.iota(iota_w[:], [[1, WIN]], base=0, channel_multiplier=0,
                   allow_small_or_imprecise_dtypes=True).then_inc(s_const, 1)
            g.iota(iota_p[:], [[0, 1]], base=0, channel_multiplier=1,
                   allow_small_or_imprecise_dtypes=True).then_inc(s_const, 1)
            g.memset(eps_col, EPS).then_inc(s_const, 1)
            g.memset(one_col, 1.0).then_inc(s_const, 1)
            g.wait_ge(s_const, 4)
            g.affine_select(out=ident[:], in_=ident[:], compare_op=ALU.not_equal, fill=1.0, base=0,
                            pattern=[[-1, P]], channel_multiplier=1).then_inc(s_const, 1)
            g.memset(w_heads, 0.0).then_inc(s_zero, 1)
            plan_gpsimd(g)
            meet(g, "pool")
            meet(g, "pool")
            gathers(g, "mlp", x, [v[:, :, 0:D] for v in xe], D, l0_a, 2, l0_g)
            meet(g, "pool")
            meet(g, "pool")
            gathers(g, "sum0", x1_d, xg, D, lin[0]["loaded"], 2, lin[0]["gathered"])
            meet(g, "pool")
            meet(g, "pool")
            gathers(g, "gat", x2_d, xa, TW, g1_a, 1, g1_g)
            meet(g, "pool")
            meet(g, "pool")

            def gat_sum_rows(it):
                for k in range(SLOTS):
                    g.wait_ge(g2["summed"], it * SLOTS + (k + 2))
                    hold(g)
                    g.dma_start(xa[k], edges_d[bass.ds((SLOTS * it + k) * CHUNK, CHUNK), :]
                                .rearrange("(p t) f -> p t f", t=TILES)).then_inc(g2_x[k], 16)
            steps(g, gat_sum_rows)
            meet(g, "pool")
            meet(g, "pool")
            gathers(g, "sum1", x3_d, xg, D, lin[1]["loaded"], 2, lin[1]["gathered"])
            meet(g, "pool")
            meet(g, "pool")
            gathers(g, "sum2", p_d, xg, D, lin[2]["loaded"], 2, lin[2]["gathered"])
            meet(g, "pool")
            meet(g, "pool")

        @block.sync
        def _(sp):
            ends = dst[1:1 + CH * CHUNK].rearrange("(c e) -> c e", e=CHUNK)
            with nc.allow_non_contiguous_dma(reason="one number per chunk"):
                sp.dma_start(ends_i[:, 0, :], ends[:, 0:1].rearrange("c o -> o c")).then_inc(s_plan_in, 16)
                sp.dma_start(ends_i[:, 1, :], ends[:, CHUNK - 1:CHUNK].rearrange("c o -> o c")).then_inc(s_plan_in, 16)
            sp.wait_ge(s_zero, 1)
            loads = [
                (xn[:], rows(x)),
                (w1_edge[0:D, :], W1[0:D, :]), (w1_dst, W1[D:2 * D, :]),
                (w1_edge[D:2 * D, :], W1[2 * D:3 * D, :]),
                (w2, W2), (s1[0:D, :], S1l), (s1[D:2 * D, :], S1r), (s2[:, 0:D], S2l), (s2[:, D:2 * D], S2r),
                (b1_col, b1.rearrange("(n o) -> n o", o=1)), (sb1_col, sb1.rearrange("(n o) -> n o", o=1)),
                (b2_row, b2.rearrange("(o n) -> o n", o=1).partition_broadcast(P)),
                (sb2_row, sb2.rearrange("(o n) -> o n", o=1).partition_broadcast(P)),
                (gat_bias_row, gat_bias.rearrange("(o n) -> o n", o=1).partition_broadcast(P)),
                (fc_b_col, fc_b.rearrange("(o n) -> o n", o=1).partition_broadcast(P)),
                (fc_rows, fc_w.partition_broadcast(D)),
                (w_fho, gat_w.rearrange("h f o -> f h o")),
            ] + [(w_heads[h * D:(h + 1) * D, h * D:(h + 1) * D], gat_w[h]) for h in range(H)]
            for to, of in loads:
                sp.dma_start(to, of).then_inc(s_in, 16)
            sp.wait_ge(s_in, 16 * len(loads))
            sp.wait_ge(s_plan_made, 2)
            with nc.allow_non_contiguous_dma(reason="plan, one number per step"):
                for r in range(2):
                    sp.dma_start(plan_d[r].rearrange("(j p) -> p j", p=P), got_i[:, r, :]).then_inc(s_plan_st, 16)
            sp.wait_ge(s_plan_st, 32)
            sp.dma_start(plan[:], plan_d.rearrange("(o r) s -> o r s", o=1)).then_inc(s_plan_ld, 16)
            sp.dma_start(base_i, plan_d[1:2, :].partition_broadcast(P)).then_inc(s_plan_ld, 16)
            sp.dma_start(base_late[:, SLOTS:SLOTS + TAB * P], plan_d[1:2, :]).then_inc(s_plan_ld, 16)
            sp.wait_ge(s_plan_ld, 48)
            meet(sp, "sp")

            sp.wait_ge(s_evac[1], SEVENS)
            sp.wait_ge(s_tail, 1)
            store(sp, rows(q_d), q_n)
            store(sp, q_d[NP:NT, :], zero_tail[:, 0:HID])
            store(sp, gat_d[NP:NT, :], zero_tail[:, 0:3 * H].bitcast(BF16))
            sp.wait_ge(s_out, stored[0])
            meet(sp, "sp")

            def mlp_loads(it):
                for k in range(SLOTS):
                    c, b = chunk_of(sp, it, k), base_of(sp, it, k)
                    sp.wait_ge(l0["hidden"], it * (SLOTS * NS) + NS * (k + 1))
                    sp.dma_start(idx[k], edge_slice(src, c)).then_inc(l0_a[k], 16)
                    sp.dma_start(xe[k][:, :, D:2 * D],
                                 edge_attr[bass.ds(c * CHUNK, CHUNK), :].rearrange("(p t) f -> p t f", t=TILES)
                                 ).then_inc(l0_a[k], 16)
                    sp.dma_start(dst_i[k], edge_slice(dst, c, 1)).then_inc(l0_b[k], 16)
                    sp.dma_start(next_i[k], edge_slice(dst, c, 2)).then_inc(l0_b[k], 16)
                    sp.dma_start(row_i[k][W0:W1_, 0:CHUNK + 1],
                                 dst[bass.ds(c * CHUNK, CHUNK + 1)].rearrange("(o e) -> o e", o=1)
                                 .partition_broadcast(WIN)).then_inc(l0_b[k], 16)
                    sp.dma_start(w_step[k][W0:W1_, :], q_d[bass.ds(b, WIN), :]).then_inc(l0_b[k], 16)
            steps(sp, mlp_loads)
            meet(sp, "sp")

            def write_x(table, width):
                sp.wait_ge(s_norm, s_norm_n["sp"] + 1)
                s_norm_n["sp"] += 1
                store(sp, rows(table)[:, :, 0:D], xn[:])

            def sum_loads(m):
                def body(it):
                    for k in range(SLOTS):
                        c = chunk_of(sp, it, k)
                        sp.wait_ge(m["added"], it * SLOTS + (k + 1))
                        sp.dma_start(idx[k], edge_slice(src, c)).then_inc(m["loaded"][k], 16)
                        sp.dma_start(dst_i[k], edge_slice(dst, c, 1)).then_inc(m["loaded"][k], 16)
                steps(sp, body)
                meet(sp, "sp")

            write_x(x1_d, D)
            sp.wait_ge(s_out, stored[0])
            meet(sp, "sp")
            sum_loads(lin[0])

            write_x(x2_d, TW)
            sp.wait_ge(s_asd, 1)
            with nc.allow_non_contiguous_dma(reason="attention columns beside each node's features"):
                store(sp, rows(x2_d)[:, :, D:TW], asd[:, :, 0:H])
            sp.wait_ge(s_out, stored[0])
            meet(sp, "sp")

            def gat_max_loads(it):
                for k in range(SLOTS):
                    c = chunk_of(sp, it, k)
                    sp.wait_ge(g1["turned"], it * (SLOTS * NS) + NS * (k + 1))
                    sp.wait_ge(g1_s[k], (it + 1) * 16)
                    sp.dma_start(idx[k], edge_slice(src, c)).then_inc(g1_a[k], 16)
                    sp.wait_ge(g1["scanned"], it * SLOTS + (k + 1))
                    sp.dma_start(dst_i[k], edge_slice(dst, c, 1)).then_inc(g1_b[k], 16)
                    sp.dma_start(next_i[k], edge_slice(dst, c, 2)).then_inc(g1_b[k], 16)
                    sp.dma_start(row4_i[k][:, 0:CHUNK + 1],
                                 dst[bass.ds(c * CHUNK, CHUNK + 1)].rearrange("(o e) -> o e", o=1)
                                 .partition_broadcast(H)).then_inc(g1_b[k], 16)
            steps(sp, gat_max_loads)
            meet(sp, "sp")

            sp.wait_ge(s_gat_tab, 1)
            store(sp, rows(gat_d), gat_parts.rearrange("p b q f -> p b (q f)"))
            sp.wait_ge(s_out, stored[0])
            meet(sp, "sp")

            def gat_sum_loads(it):
                for k in range(SLOTS):
                    c, b = chunk_of(sp, it, k), base_of(sp, it, k)
                    sp.wait_ge(g2["logit"], it * SLOTS + (k + 1))
                    sp.dma_start(dst_i[k], edge_slice(dst, c, 1)).then_inc(g2_l[k], 16)
                    sp.dma_start(row2_i[k], dst[bass.ds(c * CHUNK + 1, CHUNK)].rearrange("(o e) -> o e", o=1)
                                 .partition_broadcast(WIN)).then_inc(g2_l[k], 16)
                    sp.dma_start(gat_win[k], gat_d[bass.ds(b, WIN), :]).then_inc(g2_l[k], 16)
            steps(sp, gat_sum_loads)
            meet(sp, "sp")

            write_x(x3_d, D)
            sp.wait_ge(s_out, stored[0])
            meet(sp, "sp")
            sum_loads(lin[1])
            sp.wait_ge(s_p, 1)
            store(sp, rows(p_d), p_n)
            sp.wait_ge(s_out, stored[0])
            meet(sp, "sp")
            sum_loads(lin[2])
            sp.wait_ge(s_norm, 4)
            whole = N // P
            store(sp, out[0:whole * P, :].rearrange("(b p) f -> p b f", p=P), xn[:, 0:whole, :])
            if N % P:
                store(sp, out[whole * P:N, :], xn[0:N % P, whole, :])
            sp.wait_ge(s_out, stored[0])
            meet(sp, "sp")

        @block.tensor
        def _(pe):
            meet(pe, "pe")
            pe_groups(0, len(FOURS), turn_to_features(D, lambda b: xn[:, b, :]))
            pe.wait_ge(s_evac[0], len(FOURS))

            def q_fill(g, b):
                for j in range(7):
                    n0 = (g * 7 + j) * P
                    m = pe.matmul(b[:, j * HID:(j + 1) * HID], acc[0:D, n0:n0 + P], w1_dst, start=True, stop=True)
                return m
            pe_groups(1, SEVENS, q_fill)
            meet(pe, "pe")

            pe.sem_inc(l0["hidden"], SLOTS * NS)
            pe.wait_ge(s_ready[0], 1)

            pe.wait_ge(l0["weights"], SLOTS)

            def mlp(it):
                def turn(k):
                    pe.wait_ge(l0_g[k], (it + 1) * (16 * TILES))
                    hold(pe)
                    for j in range(NS):
                        pe.wait_ge(l0["xe_t"], it * (SLOTS * NS) + (NS * k + j + 1))
                        hold(pe)
                        for t in range(TS):
                            m = pe.transpose(bank[j][0:2 * D, t * P:(t + 1) * P], xe[k][:, TS * j + t, :], ident[:])
                        m.then_inc(l0["xe_turned"], 1)

                def products(k):
                    pe.wait_ge(l0["starts"], it * SLOTS + (k + 2))
                    pe.wait_ge(l0["xe_t"], it * (SLOTS * NS) + (NS + NS * (k + 1)))
                    for j in range(NS):
                        pe.wait_ge(l0["relu"], it * (SLOTS * NS) + (NS * k + j + 1))
                        hold(pe)
                        pe.matmul(bank[2 + j][0:HID, :], w_step[k], xo_t[k][:, j * SLICE:(j + 1) * SLICE],
                                  start=True, stop=True).then_inc(l0["hidden"], 1)

                def values(k):
                    for j in range(NS):
                        pe.wait_ge(l0["relu"], it * (SLOTS * NS) + (NS + NS * k + j + 1))
                        pe.wait_ge(l0["scanned"], it * (SLOTS * NS) + (NS * k + j + 1))
                        hold(pe)
                        pe.matmul(bank[4 + j][0:D, :], w2, hid_t[j], start=True,
                                  stop=True).then_inc(l0["values"], 1)

                def back(k):
                    pe.wait_ge(l0["scanned"], it * (SLOTS * NS) + (NS + NS * (k + 1)))
                    pe.wait_ge(l0["run_e"], it * SLOTS + (k + 2))
                    hold(pe)
                    r = run[k].rearrange("f (p t) -> f t p", t=TILES)
                    for t in range(TILES):
                        o = (k % 2) * TILES * D + t * D
                        m = pe.transpose(bank[6][:, o:o + D], r[:, t, :], ident[0:D, 0:D])
                    m.then_inc(l0["run_turned"], 1)

                def pick(k):
                    pe.wait_ge(l0["run_e"], it * SLOTS + (2 + k + 1))
                    pe.wait_ge(l0["added"], it * SLOTS + (SLOTS + k))
                    hold(pe)
                    for t in range(TILES):
                        m = pe.matmul(bank[7][0:D + 1, k * WIN:(k + 1) * WIN], run_e[k % 2][:, t, :],
                                      onehot[k][:, t, :], start=(t == 0), stop=(t == TILES - 1))
                    m.then_inc(l0["picked"], 1)

                turn(0)
                products(0)
                for k in range(SLOTS):
                    if k + 1 < SLOTS:
                        turn(k + 1)
                    values(k)
                    if k + 1 < SLOTS:
                        products(k + 1)
                    if k >= 1:
                        back(k - 1)
                    if k >= 2:
                        pick(k - 2)
                back(SLOTS - 1)
                pick(SLOTS - 2)
                pick(SLOTS - 1)
            steps(pe, mlp)
            meet(pe, "pe")
            pe_groups(2, GROUPS, turn_to_nodes(D + 1, acc))
            meet(pe, "pe")

            def sums(n):
                m_ = lin[n]
                pe.wait_ge(m_["ones"], SLOTS)

                def body(it):
                    for k in range(SLOTS):
                        pe.wait_ge(m_["gathered"][k], (it + 1) * (16 * TILES))
                        pe.wait_ge(m_["onehot"], it * SLOTS + (k + 1))
                        pe.wait_ge(m_["added"], it * SLOTS + (k + 1))
                        hold(pe)
                        for t in range(TILES):
                            m = pe.matmul(bank[k][0:D + 1, 0:WIN], xg[k][:, t, :], onehot[k][:, t, :],
                                          start=(t == 0), stop=(t == TILES - 1))
                        m.then_inc(m_["summed"], 1)
                steps(pe, body)
                meet(pe, "pe")

            sums(0)
            pe_groups(3, GROUPS, turn_to_nodes(D + 1, acc))
            pe.wait_ge(s_norm, 2)
            for g, (b0, n) in enumerate(FOURS):
                if g >= 2:
                    pe.wait_ge(s_evac[4], g - 1)
                turn_to_features(D, lambda b: xn[:, b, :])(g, bank[g % 2]).then_inc(s_turn[4], 1)
            pe.wait_ge(s_evac[4], len(FOURS))
            for b in range(NB):
                m = pe.matmul(bank[2 + b // 49][:, (b % 49) * 2 * H:(b % 49 + 1) * 2 * H],
                              acc[0:D, b * P:(b + 1) * P], wa, start=True, stop=True)
            m.then_inc(s_terms, 1)
            meet(pe, "pe")

            pe.sem_inc(g1["turned"], SLOTS * NS)
            pe.wait_ge(s_ready[2], 1)

            def gat_max(it):
                def turn(k):
                    pe.wait_ge(g1_g[k], (it + 1) * (16 * TILES))
                    hold(pe)
                    for j in range(NS):
                        pe.wait_ge(g1["ad_t"], it * (SLOTS * NS) + (NS * k + j + 1))
                        hold(pe)
                        for t in range(TS):
                            m = pe.transpose(bank[j][0:H, t * P:(t + 1) * P], xa[k][:, TS * j + t, D:TW], ident[:])
                        m.then_inc(g1["turned"], 1)

                def back(k):
                    pe.wait_ge(g1["scanned"], it * SLOTS + (SLOTS + k + 1))
                    pe.wait_ge(g1["run_e"], it * SLOTS + (k + 2))
                    hold(pe)
                    r = run4[k].rearrange("f (p t) -> f t p", t=TILES)
                    for t in range(TILES):
                        o = (k % 2) * TILES * H + t * H
                        m = pe.transpose(bank[6][:, o:o + H], r[:, t, :], ident[0:H, 0:H])
                    m.then_inc(g1["run_turned"], 1)

                def pick(k):
                    pe.wait_ge(g1["run_e"], it * SLOTS + (2 + k + 1))
                    pe.wait_ge(g1["added"], it * SLOTS + (SLOTS + k))
                    hold(pe)
                    for t in range(TILES):
                        m = pe.matmul(bank[7][0:H, k * WIN:(k + 1) * WIN], run4_e[k % 2][:, t, :],
                                      onehot[k][:, t, :], start=(t == 0), stop=(t == TILES - 1))
                    m.then_inc(g1["picked"], 1)

                for k in range(SLOTS):
                    turn(k)
                    if k >= 1:
                        back(k - 1)
                    if k >= 2:
                        pick(k - 2)
                back(SLOTS - 1)
                pick(SLOTS - 2)
                pick(SLOTS - 1)
            steps(pe, gat_max)
            meet(pe, "pe")
            for b in range(NB):
                m = pe.transpose(bank[0][:, b * H:(b + 1) * H], acc[0:H, b * P:(b + 1) * P], ident[0:H, 0:H])
            m.then_inc(s_max_n, 1)
            meet(pe, "pe")

            pe.wait_ge(s_ready[3], 2)
            pe.sem_inc(g2["spread"], 1)
            pe.sem_inc(g2["summed"], 3)
            pe.sem_inc(g2["turned"], 1)

            def spread(it, k):
                pe.wait_ge(g2["onehot_t"], it * SLOTS + (k + 1))
                pe.wait_ge(g2["logit"], it * SLOTS + (k + 1))
                hold(pe)
                o = onehot2_t[k].rearrange("w (p t) -> w t p", t=TILES)
                for t in range(TILES):
                    at_ = t * 6 * H
                    m = pe.matmul(spread_bank[k][:, at_:at_ + 6 * H], o[:, t, :], gat_win[k], start=True, stop=True)
                m.then_inc(g2["spread"], 1)

            def total(it, k):
                pe.wait_ge(g2["msg"], it * SLOTS + (k + 1))
                pe.wait_ge(g2["sum_n"], it * SLOTS + (k + 1))
                hold(pe)
                j = (k - 2) % SLOTS
                for t in range(TILES):
                    m = pe.matmul(bank[2 + k % 2][0:WIN, 0:P + H], onehot[j][:, t, :], msg[j][:, t, :],
                                  start=(t == 0), stop=(t == TILES - 1))
                m.then_inc(g2["summed"], 1)

            def back(it, k):
                pe.wait_ge(g2["sum_n"], it * SLOTS + (k + 1))
                pe.wait_ge(g2["added"], it * SLOTS + (k + 1))
                hold(pe)
                pe.transpose(bank[4 + k % 2][:, 0:WIN], sum_n[k % 2][:, 0:P], ident[0:WIN, 0:WIN])
                pe.transpose(bank[4 + k % 2][0:H, WIN:2 * WIN], sum_n[k % 2][:, P:P + H],
                             ident[0:WIN, 0:WIN]).then_inc(g2["turned"], 1)

            def gat_sum(it):
                for k in range(SLOTS):
                    back(it, k)
                    spread(it, k)
                    total(it, k)
            n = steps(pe, gat_sum)
            it = (n + (SLOTS - 1)) // SLOTS
            for k in range(SLOTS):
                back(it, k)
                if k < 2:
                    total(it, k)
            meet(pe, "pe")
            for b in range(NB):
                m = pe.transpose(bank[7][:, b * H:(b + 1) * H], den[0:H, b * P:(b + 1) * P], ident[0:H, 0:H])
            m.then_inc(s_max_n, 1)

            def heads_fill(g, b):
                b0, n = FOURS[g]
                for j in range(n):
                    m = pe.matmul(b[:, j * P:(j + 1) * P], acc[:, (b0 + j) * P:(b0 + j + 1) * P], w_heads,
                                  start=True, stop=True)
                return m
            pe_groups(5, len(FOURS), heads_fill)
            meet(pe, "pe")
            sums(1)
            pe_groups(6, GROUPS, turn_to_nodes(D + 1, acc))
            pe.wait_ge(s_cat, 1)
            pe_groups(7, len(FOURS), turn_to_features(2 * D, lambda b: cat_n[:, b, :]))
            pe.wait_ge(s_evac[7], len(FOURS))
            for g, (b0, n) in enumerate(FOURS):
                if g >= 2:
                    pe.wait_ge(s_hs, g - 1)
                pe.matmul(bank[2 + g % 2][0:HID, 0:n * P], s1, acc[0:2 * D, b0 * P:(b0 + n) * P],
                          start=True, stop=True).then_inc(s_hp, 1)
            pe.wait_ge(s_hs, len(FOURS))
            for g in range(SEVENS):
                if g >= 2:
                    pe.wait_ge(s_pr_out, g - 1)
                for j in range(7):
                    b = g * 7 + j
                    m = pe.matmul(bank[4 + g % 2][:, j * 2 * D:(j + 1) * 2 * D], hs_t[:, b * P:(b + 1) * P], s2,
                                  start=True, stop=True)
                m.then_inc(s_pr, 1)
            meet(pe, "pe")
            sums(2)
            for g in range(GROUPS):
                if g >= 2:
                    pe.wait_ge(s_fin_out, g - 1)
                turn_to_nodes(D + 1, acc)(g, bank[g % 2]).then_inc(s_fin, 1)
            meet(pe, "pe")

        @block.scalar
        def _(act):
            meet(act, "act")
            take_groups(act, 0, len(FOURS), empty_to(act_copy, acc, D))
            meet(act, "act")

            act.sem_inc(l0["xe_t"], NS)
            act.sem_inc(l0["relu"], NS)
            act.sem_inc(l0["run_e"], 2)
            for k in range(SLOTS):
                act.activation(w_step[k][0:W0, :], w1_edge, ACT.Copy).then_inc(l0["weights"], 1)

            def mlp(it):
                def row(k):
                    act.wait_ge(l0_b[k], (it + 1) * 64)
                    act.wait_ge(l0["starts"], it * SLOTS + (k + 1))
                    act.activation(row_f[:, 0:CHUNK + 1], row_i[k][W0:W0 + D, 0:CHUNK + 1], ACT.Copy,
                                   scale=-START).then_inc(l0["row_f"], 1)

                def turned(k):
                    o = xo_t[k][0:W0, :].rearrange("f (p t) -> f t p", t=TILES)
                    for j in range(NS):
                        act.wait_ge(l0["xe_turned"], it * (SLOTS * NS) + (NS * k + j + 1))
                        act.activation(o[:, TS * j:TS * (j + 1), :],
                                       bank[j][0:2 * D, :].rearrange("f (t p) -> f t p", p=P),
                                       ACT.Copy).then_inc(l0["xe_t"], 1)

                def relu(k):
                    for j in range(NS):
                        act.wait_ge(l0["hidden"], it * (SLOTS * NS) + (SLOTS * NS + NS * k + j + 1))
                        act.activation(hid_t[j], bank[2 + j][0:HID, :], ACT.Relu,
                                       bias=b1_col).then_inc(l0["relu"], 1)

                def back(k):
                    act.wait_ge(l0["run_turned"], it * SLOTS + (k + 1))
                    o = (k % 2) * TILES * D
                    act.activation(run_e[k % 2][:, :, 0:D],
                                   bank[6][:, o:o + TILES * D].rearrange("p (t f) -> p t f", f=D),
                                   ACT.Copy).then_inc(l0["run_e"], 1)

                row(0)
                turned(0)
                for k in range(SLOTS):
                    if k + 1 < SLOTS:
                        row(k + 1)
                    relu(k)
                    if k + 1 < SLOTS:
                        turned(k + 1)
                    if k >= 1:
                        back(k - 1)
                back(SLOTS - 1)
            steps(act, mlp)
            meet(act, "act")

            def root():
                n = s_root[0] = s_root[0] + 1
                act.wait_ge(s_var, n)
                act.activation(rstd, var, ACT.Sqrt, bias=eps_col, scale=1.0 / D).then_inc(s_sqrt, 1)

            root()
            meet(act, "act")
            meet(act, "act")
            root()
            take_groups(act, 4, len(FOURS), empty_to(act_copy, acc, D))
            act.wait_ge(s_terms, 1)
            for h in range(2):
                act.activation(asd[:, 49 * h:49 * (h + 1), :],
                               bank[2 + h][:, 0:49 * 2 * H].rearrange("p (b f) -> p b f", f=2 * H),
                               ACT.Copy).then_inc(s_asd_half, 1)
            act.wait_ge(s_asd_half, 2)
            act.sem_inc(s_asd, 1)
            meet(act, "act")

            act.sem_inc(g1["ad_t"], NS)
            act.sem_inc(g1["run_e"], 2)
            for k in range(SLOTS):
                act.dma_start(prime_d[k:k + 1, :], ident[0:1, 0:D]).then_inc(g1_s[k], 16)

            def gat_max(it):
                def turned(k):
                    act.wait_ge(g1_g[k], (it + 1) * (16 * TILES))
                    act.dma_start(edges_d[bass.ds((SLOTS * it + k) * CHUNK, CHUNK), :]
                                  .rearrange("(p t) f -> p t f", t=TILES), xa[k]).then_inc(g1_s[k], 16)
                    act.wait_ge(g1_b[k], (it + 1) * 48)
                    act.wait_ge(g1["starts"], it * SLOTS + (k + 1))
                    act.activation(row4_f[:, 0:CHUNK + 1], row4_i[k][:, 0:CHUNK + 1], ACT.Copy,
                                   scale=-START).then_inc(g1["row_f"], 1)
                    o = ad_t[k].rearrange("f (p t) -> f t p", t=TILES)
                    for j in range(NS):
                        act.wait_ge(g1["turned"], it * (SLOTS * NS) + (SLOTS * NS + NS * k + j + 1))
                        act.activation(o[:, TS * j:TS * (j + 1), :],
                                       bank[j][0:H, :].rearrange("f (t p) -> f t p", p=P),
                                       ACT.Copy).then_inc(g1["ad_t"], 1)

                def back(k):
                    act.wait_ge(g1["run_turned"], it * SLOTS + (k + 1))
                    o = (k % 2) * TILES * H
                    act.activation(run4_e[k % 2], bank[6][:, o:o + TILES * H].rearrange("p (t f) -> p t f", f=H),
                                   ACT.Copy).then_inc(g1["run_e"], 1)

                for k in range(SLOTS):
                    turned(k)
                    if k >= 1:
                        back(k - 1)
                back(SLOTS - 1)
            n = steps(act, gat_max)
            for k in range(SLOTS):
                act.wait_ge(g1_s[k], (n + (SLOTS - 1)) // SLOTS * 16 + 16)
                hold(act)
            meet(act, "act")
            meet(act, "act")

            act.wait_ge(s_ready[3], 2)
            act.sem_inc(g2["sum_n"], 1)
            act.sem_inc(g2["weight"], 1)

            def spread_rows(it, k):
                at_ = it * (2 * SLOTS)
                act.wait_ge(g2_l[k], (it + 1) * 48)
                act.activation(own_f, base_f[0:WIN, bass.ds(SLOTS * it + k, 1)], ACT.Identity,
                               bias=iota_p[0:WIN, :]).then_inc(g2["row"], 1)
                act.wait_ge(g2["row"], at_ + (2 * k + 1))
                act.activation(far_f, row2_i[k], ACT.Abs, bias=own_f, scale=-1.0).then_inc(g2["row"], 1)
                act.wait_ge(g2["row"], at_ + (2 * k + 2))
                act.activation(onehot2_t[k], far_f, ACT.Relu, bias=one_col[0:WIN, :],
                               scale=-1.0).then_inc(g2["onehot_t"], 1)

            def weigh(it, k):
                j = (k - 1) % SLOTS
                act.wait_ge(g2["logit"], it * SLOTS + (k + 4))
                act.wait_ge(g2["summed"], it * SLOTS + (k + 1))
                act.activation(msg[j][:, :, P:P + H], logit[j], ACT.Exp).then_inc(g2["weight"], 1)

            def empty(it, k):
                j = (k - 3) % 2
                act.wait_ge(g2["summed"], it * SLOTS + (k + 3))
                act.wait_ge(g2["turned"], it * SLOTS + (k + 1))
                act.activation(sum_n[j], bank[2 + j][0:WIN, 0:P + H], ACT.Copy).then_inc(g2["sum_n"], 1)

            def gat_sum(it):
                for k in range(SLOTS):
                    spread_rows(it, k)
                    weigh(it, k)
                    empty(it, k)
            n = steps(act, gat_sum)
            it = (n + (SLOTS - 1)) // SLOTS
            weigh(it, 0)
            for k in range(3):
                empty(it, k)
            meet(act, "act")
            root()
            meet(act, "act")
            meet(act, "act")
            take_groups(act, 7, len(FOURS), empty_to(act_copy, acc, 2 * D))
            for g, (b0, n) in enumerate(FOURS):
                act.wait_ge(s_hp, g + 1)
                act.activation(hs_t[:, b0 * P:(b0 + n) * P], bank[2 + g % 2][0:HID, 0:n * P], ACT.Relu,
                               bias=sb1_col).then_inc(s_hs, 1)
            meet(act, "act")
            meet(act, "act")
            root()
            meet(act, "act")

        @block.vector
        def _(v):
            own = Own(v, "vector_own")
            v.wait_ge(s_plan_in, 32)
            own(v.tensor_copy(ends_f, ends_i))
            own(v.tensor_tensor(more_i, ends_f[:, 1, :], ends_f[:, 0, :], ALU.subtract))
            own(v.tensor_scalar(more_i, more_i, 4, None, ALU.arith_shift_right))
            own(v.tensor_scalar(more_i, more_i, 683.0, None, ALU.mult))
            own(v.tensor_scalar(more_i, more_i, 11, None, ALU.arith_shift_right))
            own(v.tensor_scalar(row_s, more_i, 1.0, None, ALU.add))
            own(v.memset(zero_s, 1.0))
            own(v.tensor_tensor_scan(val_s, zero_s, row_s, 0.0, ALU.mult, ALU.add))
            own(v.tensor_copy(count[0:1, 0:1], val_s[:, CH - 1:CH]))
            own(v.tensor_tensor(start_s[:, 0, :], val_s, row_s, ALU.subtract))
            own(v.scalar_tensor_tensor(out=val_s, in0=start_s[:, 0, :], scalar=-float(WIN), in1=ends_f[:, 0, :],
                                       op0=ALU.mult, op1=ALU.add))
            own(v.tensor_copy(start_s[:, 1, 0:1], val_s[:, 0:1]))
            own(v.tensor_tensor(start_s[:, 1, 1:CH], val_s[:, 1:CH], val_s[:, 0:CH - 1], ALU.subtract))
            v.sem_inc(s_plan_made, 1)
            v.wait_ge(s_plan_b, 1)
            v.wait_ge(s_step, 1)
            for j in range(TAB):
                s = step_s[:, j:j + 1]
                own(v.scalar_tensor_tensor(out=hit_s, in0=start_b[:, 0, :], scalar=s, in1=start_b[:, 0, :],
                                           op0=ALU.is_le, op1=ALU.bypass))
                own(v.tensor_reduce(got_s[:, 0, j:j + 1], hit_s, AX.X, ALU.add))
                own(v.tensor_tensor(hit_s, hit_s, start_b[:, 1, :], ALU.mult))
                own(v.tensor_reduce(got_s[:, 1, j:j + 1], hit_s, AX.X, ALU.add))
            own(v.tensor_scalar(got_s[:, 0, :], got_s[:, 0, :], -1.0, None, ALU.add))
            own(v.scalar_tensor_tensor(out=got_s[:, 1, :], in0=step_s, scalar=float(WIN), in1=got_s[:, 1, :],
                                       op0=ALU.mult, op1=ALU.add))
            own(v.tensor_scalar(got_s[:, 1, :], got_s[:, 1, :], float(NP), None, ALU.min))
            own(v.tensor_copy(got_i, got_s))
            v.sem_inc(s_plan_made, 1)
            v.wait_ge(s_plan_ld, 48)
            own(v.tensor_copy(base_f[:], base_i))
            own(v.memset(val_s[:, 0:SLOTS], float(NP)))
            own(v.tensor_copy(base_late[:, 0:SLOTS], val_s[:, 0:SLOTS]))
            v.wait_ge(s_in, 16 * 21)
            for half, o in ((1, 0), (0, H)):
                own(v.tensor_tensor(wprod, w_fho, fc_rows[:, half * D:(half + 1) * D]
                                    .rearrange("p (h o) -> p h o", h=1).to_broadcast([D, H, D]), ALU.mult))
                own(v.tensor_reduce(wa[:, o:o + H], wprod, AX.X, ALU.add))
            meet(v, "dve")

            v.memset(zero_tail, 0.0).then_inc(s_tail, 1)

            def q_out(g, b):
                return v.tensor_copy(q_n[:, 7 * g:7 * g + 7, :], b[:, 0:7 * HID].rearrange("p (b f) -> p b f", f=HID))
            take_groups(v, 1, SEVENS, q_out)
            meet(v, "dve")

            def window(it, k, chain, at_, ends):
                s = base_f[:, bass.ds(SLOTS * it + k, 1)]
                v.tensor_scalar(win_f, iota_w[:], s, 1.0, ALU.add, ALU.add).then_inc(chain, 1)
                if ends:
                    v.tensor_tensor(last_f, dst_i[k], next_i[k], ALU.not_equal).then_inc(chain, 1)
                    v.wait_ge(chain, at_ + 2)
                    v.scalar_tensor_tensor(out=key_f, in0=dst_i[k], scalar=1.0, in1=last_f,
                                           op0=ALU.add, op1=ALU.mult).then_inc(chain, 1)
                    return
                v.tensor_scalar(key_f, dst_i[k], 1.0, None, ALU.add).then_inc(chain, 1)

            def compare(k):
                return v.tensor_tensor(onehot[k], key_f.rearrange("p (t o) -> p t o", o=1).to_broadcast([P, TILES, WIN]),
                                       win_f.rearrange("p (o w) -> p o w", o=1).to_broadcast([P, TILES, WIN]),
                                       ALU.is_equal)

            v.memset(acc[0:D + 1, :], 0.0).then_inc(s_ready[0], 1)
            for r in run_e:
                own(v.memset(r[:, :, D:D + 1], 1.0))
            own(v.memset(carry[:], START))
            v.wait_ge(s_ready[0], 1)
            v.sem_inc(l0["scanned"], NS)
            v.sem_inc(l0["starts"], 1)
            v.sem_inc(l0["added"], SLOTS)

            def mlp(it):
                base = it * (8 * SLOTS)

                def prepare(k):
                    at_ = base + max(8 * k - 2, 0)
                    v.wait_ge(l0_b[k], (it + 1) * 64)
                    window(it, k, l0["chain"], at_, True)
                    v.tensor_scalar(win_p[W0:W1_, :], iota_p[W0:W1_, :], base_f[W0:W1_, bass.ds(SLOTS * it + k, 1)],
                                    -float(W0), ALU.add, ALU.add).then_inc(l0["chain"], 1)
                    v.wait_ge(l0["chain"], at_ + 4)
                    compare(k).then_inc(l0["chain"], 1)
                    v.tensor_scalar(xo_t[k][W0:W1_, :], row_i[k][W0:W1_, 1:CHUNK + 1], win_p[W0:W1_, :], None,
                                    ALU.is_equal).then_inc(l0["chain"], 1)
                    v.wait_ge(l0["row_f"], it * SLOTS + (k + 1))
                    v.wait_ge(l0["chain"], at_ + 6)
                    v.tensor_tensor(starts[k], row_f[:, 0:CHUNK], row_f[:, 1:CHUNK + 1],
                                    ALU.subtract).then_inc(l0["starts"], 1)

                def scan(k):
                    at_ = base + min(8 * k + 12, 8 * SLOTS - 2)
                    c = chunk_of(v, it, k)
                    v.wait_ge(l0["starts"], it * SLOTS + (k + 2))
                    v.tensor_copy(first, carry[:, bass.ds(c, 1)]).then_inc(l0["chain"], 1)
                    v.wait_ge(l0["chain"], at_ + 1)
                    for j in range(NS):
                        v.wait_ge(l0["values"], it * (SLOTS * NS) + (NS * k + j + 1))
                        e = slice(j * SLICE, (j + 1) * SLICE)
                        v.tensor_tensor_scan(run[k][:, e], starts[k][:, e], bank[4 + j][0:D, :],
                                             first if j == 0 else run[k][:, j * SLICE - 1:j * SLICE],
                                             ALU.add, ALU.max).then_inc(l0["scanned"], 1)
                        v.wait_ge(l0["scanned"], it * (SLOTS * NS) + (NS + NS * k + j + 1))
                    v.tensor_copy(carry[:, bass.ds(c + 1, 1)], run[k][:, CHUNK - 1:CHUNK]).then_inc(l0["chain"], 1)
                    v.wait_ge(l0["chain"], at_ + 2)

                def add(k):
                    b = base_of(v, it, k)
                    v.wait_ge(l0["picked"], it * SLOTS + (k + 1))
                    v.tensor_tensor(acc[0:D + 1, bass.ds(b, WIN)], acc[0:D + 1, bass.ds(b, WIN)],
                                    bank[7][0:D + 1, k * WIN:(k + 1) * WIN], ALU.add).then_inc(l0["added"], 1)
                    v.wait_ge(l0["added"], it * SLOTS + (SLOTS + k + 1))
                    hold(v)

                prepare(0)
                for k in range(SLOTS):
                    if k + 1 < SLOTS:
                        prepare(k + 1)
                    scan(k)
                    if k >= 2:
                        add(k - 2)
                add(SLOTS - 2)
                add(SLOTS - 1)
            steps(v, mlp)
            meet(v, "dve")

            def wide(row, f=D):
                return row.rearrange("p (b o) -> p b o", o=1).to_broadcast([P, NB, f])

            def beside(row, f=D):
                return row.rearrange("p (o f) -> p o f", o=1).to_broadcast([P, NB, f])

            def layer_norm(y):
                own(v.tensor_reduce(mean, y, AX.X, ALU.add))
                own(v.tensor_scalar(mean, mean, 1.0 / D, None, ALU.mult))
                own(v.tensor_tensor(cen, y, wide(mean), ALU.subtract))
                own(v.tensor_tensor(sq, cen, cen, ALU.mult))
                v.tensor_reduce(var, sq, AX.X, ALU.add).then_inc(s_var, 1)
                s_dve_root[0] += 1
                v.wait_ge(s_sqrt, s_dve_root[0])
                own(v.reciprocal(rstd, rstd))
                v.tensor_tensor(xn[:], cen, wide(rstd), ALU.mult).then_inc(s_norm, 1)

            def take_nodes(turned, evac, width, scale=None):
                for g in range(GROUPS):
                    v.wait_ge(turned, g + 1)
                    of = bank[g % 2][:, 0:GROUP * width].rearrange("p (b f) -> p b f", f=width)
                    to = yn[:, g * GROUP:(g + 1) * GROUP, 0:width]
                    if scale is None:
                        v.tensor_copy(to, of).then_inc(evac, 1)
                    else:
                        r = scale[:, g * GROUP:(g + 1) * GROUP]
                        v.tensor_tensor(to, of, r.rearrange("p (b o) -> p b o", o=1)
                                        .to_broadcast([P, GROUP, width]), ALU.mult).then_inc(evac, 1)
                v.wait_ge(evac, GROUPS)

            take_nodes(s_turn[2], s_evac[2], D + 1)
            y = yn[:, :, 0:D]
            own(v.tensor_scalar(has, yn[:, :, D:D + 1].rearrange("p b o -> p (b o)"), -1.0, EMPTY, ALU.add, ALU.mult))
            own(v.tensor_tensor(y, y, beside(b2_row), ALU.add))
            own(v.tensor_tensor(y, y, wide(has), ALU.add))
            own(v.tensor_tensor(y, y, xn[:], ALU.max))
            own(v.tensor_tensor(y, y, xn[:], ALU.add))
            layer_norm(y)
            meet(v, "dve")

            def sums(n):
                m_ = lin[n]
                v.memset(acc[0:D + 1, :], 0.0).then_inc(m_["chain"], 1)
                for k in range(SLOTS):
                    v.memset(xg[k][:, :, D:D + 1], 1.0).then_inc(m_["ones"], 1)
                v.wait_ge(m_["chain"], 1)
                v.sem_inc(m_["added"], SLOTS)

                def body(it):
                    for k in range(SLOTS):
                        v.wait_ge(m_["loaded"][k], (it + 1) * 32)
                        window(it, k, m_["chain"], None, False)
                        v.wait_ge(m_["chain"], it * (2 * SLOTS) + (1 + 2 * k + 2))
                        compare(k).then_inc(m_["onehot"], 1)
                        v.wait_ge(m_["onehot"], it * SLOTS + (k + 1))
                    for k in range(SLOTS):
                        b = base_of(v, it, k)
                        v.wait_ge(m_["summed"], it * SLOTS + (k + 1))
                        v.tensor_tensor(acc[0:D + 1, bass.ds(b, WIN)], acc[0:D + 1, bass.ds(b, WIN)],
                                        bank[k][0:D + 1, 0:WIN], ALU.add).then_inc(m_["added"], 1)
                        v.wait_ge(m_["added"], it * SLOTS + (SLOTS + k + 1))
                    hold(v)
                steps(v, body)
                meet(v, "dve")

            sums(0)
            take_nodes(s_turn[3], s_evac[3], D + 1)
            own(v.tensor_scalar(rdeg[:], yn[:, :, D:D + 1].rearrange("p b o -> p (b o)"), 1.0, None, ALU.max))
            own(v.reciprocal(rdeg[:], rdeg[:]))
            own(v.tensor_tensor(y, y, xn[:], ALU.add))
            layer_norm(y)
            meet(v, "dve")

            v.memset(acc[:], 0.0).then_inc(s_ready[2], 1)
            own(v.memset(carry[:], START))
            v.wait_ge(s_ready[2], 1)
            v.sem_inc(g1["added"], SLOTS)
            v.sem_inc(g1["starts"], 1)
            v.sem_inc(g1["scanned"], SLOTS)

            def gat_max(it):
                base = it * (6 * SLOTS)

                def prepare(k):
                    at_ = base + 6 * k
                    v.wait_ge(g1_b[k], (it + 1) * 48)
                    window(it, k, g1["chain"], at_, True)
                    v.wait_ge(g1["chain"], at_ + 3)
                    compare(k).then_inc(g1["chain"], 1)
                    v.wait_ge(g1["row_f"], it * SLOTS + (k + 1))
                    v.wait_ge(g1["chain"], at_ + 4)
                    v.tensor_tensor(starts4[k], row4_f[:, 0:CHUNK], row4_f[:, 1:CHUNK + 1],
                                    ALU.subtract).then_inc(g1["starts"], 1)

                def scan(k):
                    at_ = base + 6 * k
                    c = chunk_of(v, it, k)
                    v.wait_ge(g1["starts"], it * SLOTS + (k + 2))
                    v.tensor_copy(first4, carry[0:H, bass.ds(c, 1)]).then_inc(g1["chain"], 1)
                    v.wait_ge(g1["chain"], at_ + 5)
                    v.wait_ge(g1["ad_t"], it * (SLOTS * NS) + (NS + NS * (k + 1)))
                    v.tensor_tensor_scan(run4[k], starts4[k], ad_t[k], first4, ALU.add,
                                         ALU.max).then_inc(g1["scanned"], 1)
                    v.wait_ge(g1["scanned"], it * SLOTS + (SLOTS + k + 1))
                    v.tensor_copy(carry[0:H, bass.ds(c + 1, 1)], run4[k][:, CHUNK - 1:CHUNK]).then_inc(g1["chain"], 1)
                    v.wait_ge(g1["chain"], at_ + 6)

                def add(k):
                    b = base_of(v, it, k)
                    v.wait_ge(g1["picked"], it * SLOTS + (k + 1))
                    v.tensor_tensor(acc[0:H, bass.ds(b, WIN)], acc[0:H, bass.ds(b, WIN)],
                                    bank[7][0:H, k * WIN:(k + 1) * WIN], ALU.add).then_inc(g1["added"], 1)
                    v.wait_ge(g1["added"], it * SLOTS + (SLOTS + k + 1))
                    hold(v)

                for k in range(SLOTS):
                    prepare(k)
                    scan(k)
                    if k >= 2:
                        add(k - 2)
                add(SLOTS - 2)
                add(SLOTS - 1)
            n = steps(v, gat_max)
            rows_before = (n + (SLOTS - 1)) // SLOTS * (16 * TILES)
            meet(v, "dve")

            v.wait_ge(s_max_n, 1)
            own(v.tensor_scalar(gat_n[:, :, 0:H], asd[:, :, H:2 * H], fc_b_col, None, ALU.add))
            own(v.tensor_tensor(gat_n[:, :, H:2 * H], gat_n[:, :, 0:H],
                                bank[0][:, 0:NB * H].rearrange("p (b f) -> p b f", f=H), ALU.add))
            own(v.tensor_scalar(gat_u, gat_n[:, :, H:2 * H], 0.2, None, ALU.mult))
            own(v.tensor_tensor(gat_n[:, :, H:2 * H], gat_n[:, :, H:2 * H], gat_u, ALU.max))
            for q in range(3):
                own(v.tensor_copy(gat_parts[:, :, q, :], gat_n))
                if q < 2:
                    own(v.tensor_tensor(gat_n, gat_n, gat_parts[:, :, q, :], ALU.subtract))
            v.sem_inc(s_gat_tab, 1)
            meet(v, "dve")

            v.memset(acc[:], 0.0).then_inc(s_ready[3], 1)
            own(v.memset(den, 0.0))
            for t in [sum_n[0]] + onehot[2:4] + xa[2:4] + msg[2:4]:
                own(v.memset(t, 0.0))
            v.sem_inc(s_ready[3], 1)
            v.wait_ge(s_ready[3], 2)
            v.sem_inc(g2["added"], 2)
            v.sem_inc(g2["logit"], 3)

            def gat_step(it, k, first, stages):
                chain = g2["chain"]
                j = (k - 1) % SLOTS
                near = near_f[j % 2]
                count_ = [0]

                def count_in(ins):
                    count_[0] += 1
                    ins.then_inc(chain, 1)
                    return first + count_[0]

                if "logits" in stages:
                    if k >= 1:
                        v.wait_ge(g2_x[j], rows_before + (it + 1) * 16)
                    v.wait_ge(g2["spread"], it * SLOTS + (k + 1))
                    spread_done = count_in(v.tensor_reduce(near, spread_bank[j][:, 0:TILES * 6 * H]
                                                           .rearrange("p (t q f) -> p t f q", q=3, f=2 * H),
                                                           AX.X, ALU.add))
                if "onehot" in stages:
                    v.wait_ge(g2_l[k], (it + 1) * 48)
                    v.wait_ge(g2["summed"], it * SLOTS + (k + 2))
                    count_in(v.scalar_tensor_tensor(
                        out=onehot[k], in0=dst_i[k].rearrange("p (t o) -> p t o", o=1).to_broadcast([P, TILES, WIN]),
                        scalar=base_f[:, bass.ds(SLOTS * it + k, 1)],
                        in1=iota_w[:].rearrange("p (o w) -> p o w", o=1).to_broadcast([P, TILES, WIN]),
                        op0=ALU.subtract, op1=ALU.is_equal))
                if "logits" in stages:
                    v.wait_ge(chain, spread_done)
                    plain = count_in(v.tensor_tensor(logit[j], xa[j][:, :, D:TW], near[:, :, 0:H], ALU.add))
                    v.wait_ge(chain, plain)
                    leaky = count_in(v.scalar_tensor_tensor(out=logit[j], in0=logit[j], scalar=0.2, in1=logit[j],
                                                            op0=ALU.mult, op1=ALU.max))
                    v.wait_ge(chain, leaky)
                    v.tensor_tensor(logit[j], logit[j], near[:, :, H:2 * H], ALU.subtract).then_inc(g2["logit"], 1)
                if "messages" in stages:
                    j = (k - 2) % SLOTS
                    v.wait_ge(g2["weight"], it * SLOTS + (k + 1))
                    v.tensor_tensor(msg[j][:, :, 0:P].rearrange("p t (h f) -> p t h f", f=D),
                                    xa[j][:, :, 0:D].rearrange("p t (o f) -> p t o f", o=1)
                                    .to_broadcast([P, TILES, H, D]),
                                    msg[j][:, :, P:P + H].rearrange("p t (h o) -> p t h o", o=1)
                                    .to_broadcast([P, TILES, H, D]), ALU.mult).then_inc(g2["msg"], 1)
                b = v.value_load(base_late[0:1, bass.ds(SLOTS * it + k, 1)], min_val=0, max_val=NP)
                v.wait_ge(g2["turned"], it * SLOTS + (k + 2))
                v.wait_ge(g2["added"], it * SLOTS + (k + 2))
                if "logits" not in stages:
                    v.wait_ge(chain, first)
                hold(v)
                count_in(v.tensor_tensor(den[:, bass.ds(b, WIN)], den[:, bass.ds(b, WIN)],
                                         bank[4 + k % 2][0:H, WIN:2 * WIN], ALU.add))
                v.tensor_tensor(acc[:, bass.ds(b, WIN)], acc[:, bass.ds(b, WIN)],
                                bank[4 + k % 2][:, 0:WIN], ALU.add).then_inc(g2["added"], 1)
                return count_[0]

            def gat_sum(it):
                at_ = 0
                for k in range(SLOTS):
                    at_ += gat_step(it, k, it * (5 * SLOTS) + at_, ("onehot", "logits", "messages"))
                v.wait_ge(g2_x[SLOTS - 1], rows_before + (it + 1) * 16)
                hold(v)
                assert at_ == 5 * SLOTS
            n = steps(v, gat_sum)
            it = (n + (SLOTS - 1)) // SLOTS
            at_ = 0
            for k in range(SLOTS):
                left = ("logits",) * (k < 1) + ("messages",) * (k < 2)
                at_ += gat_step(it, k, it * (5 * SLOTS) + at_, left)
            meet(v, "dve")

            v.wait_ge(s_max_n, 2)
            own(v.tensor_scalar(gat_u, bank[7][:, 0:NB * H].rearrange("p (b f) -> p b f", f=H), 1e-30, None, ALU.max))
            own(v.reciprocal(gat_u, gat_u))
            own(v.tensor_scalar(gat_u, gat_u, 1.0 / H, None, ALU.mult))
            for g, (b0, n) in enumerate(FOURS):
                v.wait_ge(s_turn[5], g + 1)
                t4 = heads_tmp[g % 2][:, 0:n * P]
                v.tensor_tensor(t4.rearrange("p (a o) -> p a o", o=D),
                                bank[g % 2][:, 0:n * P].rearrange("p (a o) -> p a o", o=D),
                                gat_u[:, b0:b0 + n, :].rearrange("p b (h o) -> p (b h) o", o=1)
                                .to_broadcast([P, n * H, D]), ALU.mult).then_inc(s_evac[5], 1)
                v.wait_ge(s_evac[5], g + 1)
                own(v.tensor_reduce(yn[:, b0:b0 + n, 0:D], t4.rearrange("p (b h o) -> p b o h", h=H, o=D),
                                    AX.X, ALU.add))
            own(v.tensor_tensor(y, y, beside(gat_bias_row), ALU.add))
            own(v.tensor_tensor(y, y, xn[:], ALU.add))
            layer_norm(y)
            meet(v, "dve")

            sums(1)
            take_nodes(s_turn[6], s_evac[6], D + 1, rdeg)
            own(v.tensor_copy(cat_n[:, :, 0:D], y))
            v.tensor_copy(cat_n[:, :, D:2 * D], xn[:]).then_inc(s_cat, 1)
            for g in range(SEVENS):
                v.wait_ge(s_pr, g + 1)
                of = bank[4 + g % 2][:, 0:7 * 2 * D].rearrange("p (b f) -> p b f", f=2 * D)
                own(v.tensor_copy(p_n[:, 7 * g:7 * g + 7, :], of[:, :, 0:D]))
                v.tensor_copy(res_n[:, 7 * g:7 * g + 7, :], of[:, :, D:2 * D]).then_inc(s_pr_out, 1)
            v.wait_ge(s_pr_out, SEVENS)
            v.sem_inc(s_p, 1)
            own(v.tensor_tensor(res_n, res_n, beside(sb2_row), ALU.add))
            own(v.tensor_tensor(xn[:], res_n, xn[:], ALU.add))
            meet(v, "dve")
            sums(2)
            take_nodes(s_fin, s_fin_out, D + 1, rdeg)
            own(v.tensor_tensor(y, y, xn[:], ALU.add))
            layer_norm(y)
            meet(v, "dve")



_OUT = (12500, 32)


def kernel(**inputs):
    import numpy as np
    import concourse.bacc as bacc
    from concourse.bass_utils import run_bass_kernel_spmd

    n, e = _OUT[0], inputs["src"].shape[0]
    chunks, _ = sizes(n, e)
    pad_n = -(-n // P) * P - n
    pad_e = chunks * CHUNK - e
    arrays = {
        "x": np.pad(np.asarray(inputs["x"]), ((0, pad_n), (0, 0))),
        "src": np.pad(np.asarray(inputs["src"]), (0, pad_e)),
        "dst": np.concatenate([np.full(1, -1, np.int32), np.asarray(inputs["dst"]), np.full(pad_e, n, np.int32),
                               np.full(1, n, np.int32)]),
        "edge_attr": np.pad(np.asarray(inputs["edge_attr_32"]), ((0, pad_e), (0, 0))),
    }
    for name in ("L0_gnn_W1", "L0_gnn_b1", "L0_gnn_W2", "L0_gnn_b2", "L2_gnn_w", "L2_gnn_fc_w", "L2_gnn_fc_b",
                 "L2_gnn_bias", "L3_gnn_W1_l", "L3_gnn_b1", "L3_gnn_W1_r", "L3_gnn_W2_l", "L3_gnn_b2", "L3_gnn_W2_r"):
        arrays[name] = np.ascontiguousarray(inputs[name])
    nc = bacc.Bacc("TRN2", target_bir_lowering=False, num_devices=1)
    args = [nc.dram_tensor(k, v.shape, mybir.dt.from_np(v.dtype), kind="ExternalInput").ap() for k, v in arrays.items()]
    out = nc.dram_tensor("out", _OUT, F32, kind="ExternalOutput").ap()
    gnn(nc, *args, out, e)
    r = run_bass_kernel_spmd(nc, [arrays], core_ids=[0])
    return r.results[0]["out"]
```
